# Optimizing a Trainium2 kernel written in Bass

```python
import numpy as np
import jax
import jax.numpy as jnp

def _softmax(x, axis=-1):
    return jax.nn.softmax(x, axis=axis)

def _gelu(x):
    return jax.nn.gelu(x, approximate=True)

def _silu(x):
    return jax.nn.silu(x)

def _sigmoid(x):
    return jax.nn.sigmoid(x)

def _layernorm(x, axis=-1, eps=1e-05):
    m = jnp.mean(x, axis=axis, keepdims=True)
    v = jnp.var(x, axis=axis, keepdims=True)
    return (x - m) / jnp.sqrt(v + eps)

def _scatter_add(tgt, idx, src, axis=0):
    return tgt.at[idx].add(src)

def _segment_sum(src, seg, n):
    return jax.ops.segment_sum(src, seg, n)
kernel_name = 'mk_gnn_preln_d1_gnn_r8_5a7bb6'

def setup_inputs(seed: int=0):
    np.random.seed(seed)
    _w = jnp.asarray

    def _rec_inputs():
        import jax
        import jax.numpy as jnp
        _gk = jax.random.key(seed)
        x = 0.0001712 + 1 * jax.random.normal(jax.random.fold_in(_gk, 1), (12500, 16), jnp.float32)
        src = jax.random.randint(jax.random.fold_in(_gk, 2), (400000,), 0, 12500, jnp.int32)
        dst = jax.random.randint(jax.random.fold_in(_gk, 3), (400000,), 0, 12500, jnp.int32)
        _o = jnp.argsort(dst, stable=True)
        src = src[_o]
        dst = dst[_o]
        edge_attr_8 = 0.000714719 + 1.00021 * jax.random.normal(jax.random.fold_in(_gk, 11), (400000, 8), jnp.float32)
        return (x, src, dst, edge_attr_8)
    x, src, dst, edge_attr_8 = _rec_inputs()

    def _L0_gnn_setup():
        import jax, jax.numpy as jnp
        import numpy as np
        N_NODES = 6250
        N_EDGES = 50000
        D = 16
        E_FEAT = 8
        N_LAYERS = 3
        BN_EPS = 1e-05

        def _nnconv(x, src, dst, edge_attr, ew, eb, rw, rb):
            W = (edge_attr @ ew + eb).reshape(edge_attr.shape[0], x.shape[1], rw.shape[1])
            xj = x[src]
            msg = jnp.einsum('ei,eio->eo', xj, W)
            agg = jax.ops.segment_sum(msg, dst, num_segments=x.shape[0])
            return agg + x @ rw + rb

        def _batchnorm(x, gamma, beta):
            mean = jnp.mean(x, axis=0)
            var = jnp.mean(jnp.square(x - mean), axis=0)
            return (x - mean) * jax.lax.rsqrt(var + BN_EPS) * gamma + beta
        key = jax.random.key(seed)
        ks = jax.random.split(key, 12)
        x = jax.random.normal(ks[0], (N_NODES, D), dtype=jnp.float32)
        edge_index = jax.random.randint(ks[1], (2, N_EDGES), 0, N_NODES, dtype=jnp.int64)
        edge_attr = jax.random.normal(ks[2], (N_EDGES, E_FEAT), dtype=jnp.float32)
        s = 0.1
        edge_w = jax.random.normal(ks[3], (N_LAYERS, E_FEAT, D * D), dtype=jnp.float32) * s
        edge_b = jax.random.normal(ks[4], (N_LAYERS, D * D), dtype=jnp.float32) * s
        root_w = jax.random.normal(ks[5], (N_LAYERS, D, D), dtype=jnp.float32) * s
        root_b = jax.random.normal(ks[6], (N_LAYERS, D), dtype=jnp.float32) * s
        bn_gamma = jnp.ones((N_LAYERS - 1, D), dtype=jnp.float32)
        bn_beta = jnp.zeros((N_LAYERS - 1, D), dtype=jnp.float32)
        pred_w = jax.random.normal(ks[7], (D, D), dtype=jnp.float32) * s
        pred_b = jax.random.normal(ks[8], (D,), dtype=jnp.float32) * s
        return {'x': x, 'edge_index': edge_index, 'edge_attr': edge_attr, 'edge_w': edge_w, 'edge_b': edge_b, 'root_w': root_w, 'root_b': root_b, 'bn_gamma': bn_gamma, 'bn_beta': bn_beta, 'pred_w': pred_w, 'pred_b': pred_b}
    _L0_gnn_all = _L0_gnn_setup()
    _L0_gnn_in = {k: v for k, v in _L0_gnn_all.items() if k in ('edge_w', 'edge_b', 'root_w', 'root_b', 'bn_gamma', 'bn_beta', 'pred_w', 'pred_b')}
    del _L0_gnn_all
    return {'x': x, 'src': src, 'dst': dst, 'edge_attr_8': edge_attr_8, 'L0_gnn_edge_w': _L0_gnn_in['edge_w'], 'L0_gnn_edge_b': _L0_gnn_in['edge_b'], 'L0_gnn_root_w': _L0_gnn_in['root_w'], 'L0_gnn_root_b': _L0_gnn_in['root_b'], 'L0_gnn_bn_gamma': _L0_gnn_in['bn_gamma'], 'L0_gnn_bn_beta': _L0_gnn_in['bn_beta'], 'L0_gnn_pred_w': _L0_gnn_in['pred_w'], 'L0_gnn_pred_b': _L0_gnn_in['pred_b']}

def reference(x, src, dst, edge_attr_8, L0_gnn_edge_w, L0_gnn_edge_b, L0_gnn_root_w, L0_gnn_root_b, L0_gnn_bn_gamma, L0_gnn_bn_beta, L0_gnn_pred_w, L0_gnn_pred_b):
    import jax
    import jax.numpy as jnp

    def _L0_gnn_ref(x, edge_index, edge_attr, edge_w, edge_b, root_w, root_b, bn_gamma, bn_beta, pred_w, pred_b):
        import jax, jax.numpy as jnp
        import numpy as np
        N_NODES = 6250
        N_EDGES = 50000
        D = 16
        E_FEAT = 8
        N_LAYERS = 3
        BN_EPS = 1e-05

        def _nnconv(x, src, dst, edge_attr, ew, eb, rw, rb):
            W = (edge_attr @ ew + eb).reshape(edge_attr.shape[0], x.shape[1], rw.shape[1])
            xj = x[src]
            msg = jnp.einsum('ei,eio->eo', xj, W)
            agg = jax.ops.segment_sum(msg, dst, num_segments=x.shape[0])
            return agg + x @ rw + rb

        def _batchnorm(x, gamma, beta):
            mean = jnp.mean(x, axis=0)
            var = jnp.mean(jnp.square(x - mean), axis=0)
            return (x - mean) * jax.lax.rsqrt(var + BN_EPS) * gamma + beta
        src, dst = (edge_index[0], edge_index[1])
        h = x
        for i in range(N_LAYERS - 1):
            h = _nnconv(h, src, dst, edge_attr, edge_w[i], edge_b[i], root_w[i], root_b[i])
            h = _batchnorm(h, bn_gamma[i], bn_beta[i])
            h = jax.nn.relu(h)
        h = _nnconv(h, src, dst, edge_attr, edge_w[-1], edge_b[-1], root_w[-1], root_b[-1])
        h = jax.nn.relu(h)
        return h @ pred_w + pred_b
    edge_index = jnp.stack([src, dst])
    h = jnp.maximum(_layernorm(x, axis=-1), 0.0)
    x = x + _L0_gnn_ref(h, edge_index, edge_attr_8, L0_gnn_edge_w, L0_gnn_edge_b, L0_gnn_root_w, L0_gnn_root_b, L0_gnn_bn_gamma, L0_gnn_bn_beta, L0_gnn_pred_w, L0_gnn_pred_b)
    return x

_drawn_inputs = setup_inputs


def setup_inputs(seed=0):
    import zlib

    import numpy as np

    out = dict(_drawn_inputs(seed))
    spreads = {'L0_gnn_bn_gamma': (1.0, 0.2), 'L0_gnn_bn_beta': (0.0, 0.1)}
    factors = {'L0_gnn_root_b': 7.314}
    for name, (base, spread) in spreads.items():
        noise = np.random.default_rng([zlib.crc32(name.encode()), seed]).standard_normal(out[name].shape)
        drawn = base * np.exp(spread * noise) if base else spread * noise
        out[name] = jnp.asarray(drawn.astype(out[name].dtype))
    for name, factor in factors.items():
        out[name] = (out[name] * factor).astype(out[name].dtype)
    return out
```

```python
from contextlib import ExitStack

import concourse.bass as bass
from concourse import mybir

P = 128
ALU = mybir.AluOpType
ACT = mybir.ActivationFunctionType
AX_X = mybir.AxisListType.X
F32 = mybir.dt.float32
I32 = mybir.dt.int32
RMAX = bass.bass_isa.ReduceOp.max

TILES = 25
SLOTS = 5
HOTS = 3
WIN = 128
NODE_P = 125
SUB = 4
LN_EPS = 1e-5
BN_EPS = 1e-5
CREDIT = SLOTS


def gnn_kernel(nc, x, src, dst, edge_attr, edge_w, edge_b, root_w, root_b, gamma, beta, pred_w, pred_b, out):
    N, D = x.shape
    E, F = edge_attr.shape
    L = edge_w.shape[0]
    FD = F * D
    GE = P * TILES
    G = E // GE
    BODIES = G // SLOTS
    PER = N // NODE_P
    CHUNKS = PER // SUB
    CN = NODE_P * SUB
    WINDOWS = -(-N // WIN)
    assert E == G * GE and G == BODIES * SLOTS and FD == P and D * (F + 1) <= 512
    assert N == NODE_P * PER and PER == CHUNKS * SUB and CHUNKS % SLOTS == 0 and CN <= 512

    table = nc.dram_tensor("node_table", [N, D], F32, kind="Internal").ap()
    src_g = src.rearrange("(g p j) -> g p j", p=P, j=TILES)
    ea_g = edge_attr.rearrange("(g p j) f -> g p j f", p=P, j=TILES)
    dst_all = dst.rearrange("(g p j) -> p g j", p=P, j=TILES)

    with ExitStack() as ctx:
        def sb(name, shape, dt=F32):
            return ctx.enter_context(nc.sbuf_tensor(name, shape, dt))

        def ps(name, shape):
            return ctx.enter_context(nc.psum_tensor(name, shape, F32))

        def sem(name):
            return ctx.enter_context(nc.semaphore(name))

        idx = [sb(f"idx{u}", [P, TILES], I32) for u in range(SLOTS)]
        ea = [sb(f"ea{u}", [P, TILES, F]) for u in range(SLOTS)]
        xp = [sb(f"xp{u}", [P, TILES, D + FD]) for u in range(SLOTS)]
        hot = [sb(f"hot{i}", [P, TILES, WIN]) for i in range(HOTS)]
        dst_rel = sb("dst_rel", [P, G, TILES])
        base_i = sb("base_i", [P, G], I32)
        far_i = sb("far_i", [P, 1], I32)
        agg = sb("agg", [D, N + WIN])
        rows = sb("rows", [NODE_P, PER, D])
        x_nm = sb("x_nm", [NODE_P, PER, D])
        stage = [sb(f"stage{u}", [NODE_P, SUB, D]) for u in range(SLOTS)]
        hT = [sb(f"hT{u}", [D, SUB, NODE_P]) for u in range(SLOTS)]
        w_all = sb("w_all", [P, L, D])
        eb_all = sb("eb_all", [D, L, D])
        rw_all = sb("rw_all", [D, L, D])
        rb_all = sb("rb_all", [D, L])
        w_now = sb("w_now", [P, D])
        eb_now = sb("eb_now", [D, D])
        rw_now = sb("rw_now", [D, D])
        gam = sb("gam", [D, L - 1])
        bet = sb("bet", [D, L - 1])
        pw = sb("pw", [D, D])
        pb = sb("pb", [NODE_P, D])
        col_i = sb("col_i", [P, P], I32)
        row_i = sb("row_i", [P, 1], I32)
        col = sb("col", [P, P])
        row = sb("row", [P, 1])
        ident = sb("ident", [P, P])
        eps = sb("eps", [P, 1])
        zT = sb("zT", [P, WIN])
        zxT = sb("zxT", [D, WIN])
        low_p = sb("low_p", [P, G])
        low_a = sb("low_a", [P, G])
        far_p = sb("far_p", [P, 1])
        far_a = sb("far_a", [P, 1])
        ln_m = sb("ln_m", [NODE_P, PER])
        ln_v = sb("ln_v", [NODE_P, PER])
        ln_r = sb("ln_r", [NODE_P, PER])
        bn_s = sb("bn_s", [D, CHUNKS, 6])
        bn_m = sb("bn_m", [D, 2])
        bn_d = sb("bn_d", [D, 1])
        bn_r = sb("bn_r", [D, 1])
        bn_a = sb("bn_a", [D, 1])
        bn_t = sb("bn_t", [D, 1])
        bn_b = sb("bn_b", [D, 1])
        far_idx = sb("far_idx", [P, TILES], I32)
        far_ea = sb("far_ea", [P, TILES, F])
        far_rel = sb("far_rel", [P, TILES])
        far_col = sb("far_col", [P, 1])
        far_col_i = sb("far_col_i", [P, 1], I32)

        bank = [ps(f"bank{i}", [P, 512]) for i in range(7)]
        p_z, p_zx, p_agg = bank[0][:, 0:WIN], bank[1][0:D, 0:WIN], bank[2][0:D, 0:WIN]
        p_t = [bank[i][0:NODE_P, 0:SUB * D].rearrange("p (m d) -> p m d", d=D) for i in range(3)]
        p_h, *p_r = [bank[i][0:D, 0:CN].rearrange("d (m p) -> d m p", m=SUB) for i in range(3, 7)]

        s_const = sem("const_loaded")
        s_dst = sem("dst_loaded")
        s_iota = sem("iota_done")
        s_v = sem("vector_step")
        s_low = sem("low_ready")
        s_lowall = sem("low_reduced")
        s_far = sem("far_ready")
        s_farall = sem("far_reduced")
        s_flag = sem("flag_ready")
        s_ident = sem("ident_ready")
        s_var = sem("variance_ready")
        s_std = sem("std_ready")
        s_rows = sem("rows_ready")
        s_table = sem("table_written")
        s_w = sem("weights_set")
        s_stats = sem("chunk_stats")
        s_bn = sem("norm_ready")
        s_stage = sem("chunk_staged")
        s_chT = sem("chunk_transposed")
        s_hT = sem("chunk_normed")
        s_root = sem("chunk_products")
        s_node = sem("chunk_done")
        s_idx = [sem(f"edges_loaded{u}") for u in range(SLOTS)]
        s_gath = [sem(f"gathered{u}") for u in range(SLOTS)]
        s_hot = sem("onehot_ready")
        s_prod = sem("products_ready")
        s_seg = sem("segments_summed")
        s_zT = sem("segments_copied")
        s_mm = sem("messages_ready")
        s_add = sem("messages_added")
        s_out = sem("output_written")
        s_mark = sem("wait_passed")
        s_fgo = sem("far_group_begun")
        s_fload = sem("far_edges_loaded")
        s_fgath = sem("far_gathered")
        s_fprod = sem("far_products_ready")
        s_fv = sem("far_vector_step")
        s_fhot = sem("far_onehot_ready")
        s_fseg = sem("far_segments_summed")
        s_fzT = sem("far_segments_copied")
        s_fmm = sem("far_messages_ready")
        s_fadd = sem("far_messages_added")

        block = ctx.enter_context(nc.Block())

        def chunk_of(c):
            return agg[:, 0:N].rearrange("d (p m) -> d m p", m=PER)[:, bass.ds(c * SUB, SUB), :]

        def node_chunks(eng, n0):
            with eng.Fori(0, CHUNKS // SLOTS) as cb:
                for u in range(SLOTS):
                    yield cb * SLOTS + u, u, n0 + cb * SLOTS + u

        def apart(eng):
            eng.sem_inc(s_mark, 1)

        FAR = WINDOWS - 1

        def farthest(eng):
            eng.wait_ge(s_flag, 1)
            return eng.value_load(far_i[0:1, 0:1], min_val=0, max_val=N)

        @block.sync
        def _(sp):
            sp.dma_start(dst_rel[:].bitcast(I32), dst_all).then_inc(s_dst, 16)
            sp.dma_start(x_nm[:], x.rearrange("(p m) d -> p m d", m=PER)).then_inc(s_const, 16)
            sp.dma_start(w_all[:], edge_w.rearrange("l f (i o) -> (f i) l o", o=D)).then_inc(s_const, 16)
            sp.dma_start(eb_all[:], edge_b.rearrange("l (i o) -> i l o", o=D)).then_inc(s_const, 16)
            sp.dma_start(rw_all[:], root_w.rearrange("l i o -> i l o")).then_inc(s_const, 16)
            sp.dma_start(rb_all[:], root_b).then_inc(s_const, 16)
            sp.dma_start(gam[:], gamma).then_inc(s_const, 16)
            sp.dma_start(bet[:], beta).then_inc(s_const, 16)
            sp.dma_start(pw[:], pred_w).then_inc(s_const, 16)
            sp.dma_start(pb[:], pred_b[None, :].to_broadcast([NODE_P, D])).then_inc(s_const, 16)

            sp.wait_ge(s_rows, 1)
            sp.dma_start(table.rearrange("(p m) d -> p m d", m=PER), rows[:]).then_inc(s_table, 16)

            far = farthest(sp)

            def load_far(layer):
                with sp.Fori(0, G) as g:
                    n = layer * G + g
                    sp.wait_ge(s_fgo, n + 1)
                    sp.dma_start(far_idx[:], src_g[bass.ds(g, 1), :, :]
                                 .rearrange("g p j -> (g p) j")).then_inc(s_fload, 16)
                    sp.dma_start(far_ea[:], ea_g[bass.ds(g, 1), :, :, :]
                                 .rearrange("g p j f -> (g p) j f")).then_inc(s_fload, 16)

            def load_edges(layer):
                with sp.Fori(0, BODIES) as b:
                    for u in range(SLOTS):
                        sp.wait_ge(s_prod, layer * G + b * SLOTS + (u + 1))
                        sp.dma_start(idx[u][:], src_g[bass.ds(b * SLOTS + u, 1), :, :]
                                     .rearrange("g p j -> (g p) j")).then_inc(s_idx[u], 16)
                        sp.dma_start(ea[u][:], ea_g[bass.ds(b * SLOTS + u, 1), :, :, :]
                                     .rearrange("g p j f -> (g p) j f")).then_inc(s_idx[u], 16)
                with sp.If(far > WIN - 1):
                    load_far(layer)
                sp.sem_inc(s_mark, 1)

            with sp.Fori(0, L - 1) as layer:
                load_edges(layer)
                sp.wait_ge(s_rows, layer + 2)
                sp.dma_start(table.rearrange("(p m) d -> p m d", m=PER), rows[:]).then_inc(s_table, 16)
            load_edges(L - 1)
            sp.wait_ge(s_rows, L + 1)
            sp.dma_start(out.rearrange("(p m) d -> p m d", m=PER), rows[:]).then_inc(s_out, 16)
            sp.wait_ge(s_out, 16)

        @block.gpsimd
        def _(pool):
            pool.iota(col_i[:], [[1, P]], base=0, channel_multiplier=0).then_inc(s_iota, 1)
            pool.iota(row_i[:], [[0, 1]], base=0, channel_multiplier=1).then_inc(s_iota, 1)
            pool.wait_ge(s_low, 1)
            pool.partition_all_reduce(low_a[:], low_p[:], P, RMAX).then_inc(s_lowall, 1)
            pool.wait_ge(s_far, 1)
            pool.partition_all_reduce(far_a[:], far_p[:], P, RMAX).then_inc(s_farall, 1)

            far = farthest(pool)

            def gather_far(layer):
                with pool.Fori(0, G) as g:
                    pool.wait_ge(s_fload, (layer * G + g) * 32 + 32)
                    apart(pool)
                    for j in range(TILES):
                        pool.indirect_dma_start(
                            out=xp[0][:, j, 0:D], out_offset=None, in_=table[:, :],
                            in_offset=bass.IndirectOffsetOnAxis(ap=far_idx[:, j:j + 1], axis=0),
                        ).then_inc(s_fgath, 16)

            def gather(layer):
                pool.wait_ge(s_table, layer * 16 + 16)
                apart(pool)
                with pool.Fori(0, BODIES) as b:
                    for u in range(SLOTS):
                        pool.wait_ge(s_idx[u], (layer * BODIES + b) * 32 + 32)
                        pool.wait_ge(s_seg, layer * G + b * SLOTS + (u + 1))
                        apart(pool)
                        for j in range(TILES):
                            pool.indirect_dma_start(
                                out=xp[u][:, j, 0:D], out_offset=None, in_=table[:, :],
                                in_offset=bass.IndirectOffsetOnAxis(ap=idx[u][:, j:j + 1], axis=0),
                            ).then_inc(s_gath[u], 16)
                with pool.If(far > WIN - 1):
                    gather_far(layer)
                pool.sem_inc(s_mark, 1)

            with pool.Fori(0, L - 1) as layer:
                gather(layer)
            gather(L - 1)

        @block.vector
        def _(dve):
            steps = [0]

            def step(ins):
                steps[0] += 1
                ins.then_inc(s_v, 1)
                dve.wait_ge(s_v, steps[0])

            for _ in range(CREDIT):
                dve.sem_inc(s_prod, 1)
                dve.sem_inc(s_add, 1)
                dve.sem_inc(s_node, 1)
            dve.wait_ge(s_iota, 2)
            nc.vector.tensor_copy(col[:], col_i[:])
            nc.vector.memset(eps[:], LN_EPS)
            nc.vector.memset(agg[:, N:N + WIN], 0.0)
            step(nc.vector.tensor_copy(row[:], row_i[:]))
            nc.vector.tensor_scalar(ident[:], col[:], row[:, 0:1], None, ALU.is_equal).then_inc(s_ident, 1)

            dve.wait_ge(s_const, 9 * 16)
            step(nc.vector.tensor_reduce(ln_m[:], x_nm[:], AX_X, ALU.add))
            step(nc.vector.tensor_scalar(ln_m[:], ln_m[:], 1.0 / D, None, ALU.mult))
            ln_mb = ln_m[:].unsqueeze(2).to_broadcast([NODE_P, PER, D])
            step(nc.vector.tensor_tensor(rows[:], x_nm[:], ln_mb, ALU.subtract))
            squares = hot[0][0:NODE_P, :, :].rearrange("p a b -> p (a b)")[:, 0:PER * D].rearrange("p (m d) -> p m d", d=D)
            step(nc.vector.tensor_tensor(squares, rows[:], rows[:], ALU.mult))
            nc.vector.tensor_reduce(ln_v[:], squares, AX_X, ALU.add).then_inc(s_var, 1)
            dve.wait_ge(s_std, 1)
            step(nc.vector.reciprocal(ln_r[:], ln_v[:]))
            ln_rb = ln_r[:].unsqueeze(2).to_broadcast([NODE_P, PER, D])
            step(nc.vector.tensor_tensor(rows[:], rows[:], ln_rb, ALU.mult))
            nc.vector.tensor_scalar(rows[:], rows[:], 0.0, None, ALU.max).then_inc(s_rows, 1)

            dve.wait_ge(s_dst, 16)
            step(nc.vector.tensor_copy(dst_rel[:], dst_rel[:].bitcast(I32)))
            step(nc.vector.tensor_reduce(low_p[:], dst_rel[:], AX_X, ALU.min))
            nc.vector.tensor_scalar(low_p[:], low_p[:], -1.0, None, ALU.mult).then_inc(s_low, 1)
            dve.wait_ge(s_lowall, 1)
            step(nc.vector.tensor_scalar(low_a[:], low_a[:], -1.0, None, ALU.mult))
            step(nc.vector.tensor_copy(base_i[:], low_a[:]))
            low_b = low_a[:].unsqueeze(2).to_broadcast([P, G, TILES])
            step(nc.vector.tensor_tensor(dst_rel[:], dst_rel[:], low_b, ALU.subtract))
            nc.vector.tensor_reduce(far_p[:], dst_rel[:].rearrange("p g j -> p (g j)"), AX_X,
                                    ALU.max).then_inc(s_far, 1)
            dve.wait_ge(s_farall, 1)
            step(nc.vector.tensor_copy(far_i[:], far_a[:]))
            dve.sem_inc(s_flag, 1)
            far = farthest(dve)

            def set_weights(layer):
                nc.vector.tensor_copy(w_now[:], w_all[:, bass.ds(layer, 1), :].rearrange("p l o -> p (l o)"))
                nc.vector.tensor_copy(eb_now[:], eb_all[:, bass.ds(layer, 1), :].rearrange("p l o -> p (l o)"))
                nc.vector.tensor_copy(rw_now[:], rw_all[:, bass.ds(layer, 1), :].rearrange("p l o -> p (l o)")
                                      ).then_inc(s_w, 1)

            def root_sum(layer, c, i):
                nc.vector.tensor_scalar(chunk_of(c), p_r[i], rb_all[:, bass.ds(layer, 1)], None,
                                        ALU.add).then_inc(s_node, 1)

            def segments_far(layer):
                with dve.Fori(0, G) as g:
                    n = layer * G + g
                    done = n * (1 + 3 * FAR)
                    dve.sem_inc(s_fgo, 1)
                    nc.vector.tensor_copy(far_rel[:], dst_rel[:, bass.ds(g, 1), :].rearrange("p g j -> p (g j)"))
                    nc.vector.tensor_copy(far_col[:], low_a[:, bass.ds(g, 1)]).then_inc(s_fv, 1)
                    dve.wait_ge(s_fload, n * 32 + 32)
                    dve.wait_ge(s_fgath, n * (16 * TILES) + 16 * TILES)
                    products(xp[0], far_ea).then_inc(s_fprod, 1)
                    with dve.Fori(0, FAR) as w:
                        m = n * FAR + w
                        dve.wait_ge(s_fv, done + w * 3 + 1)
                        nc.vector.tensor_scalar(far_rel[:], far_rel[:], -float(WIN), None, ALU.add).then_inc(s_fv, 1)
                        nc.vector.tensor_scalar(far_col[:], far_col[:], float(WIN), float(N), ALU.add,
                                                ALU.min).then_inc(s_fv, 1)
                        dve.wait_ge(s_fv, done + w * 3 + 3)
                        onehots(hot[0], far_rel[:]).then_inc(s_fhot, 1)
                        nc.vector.tensor_copy(far_col_i[:], far_col[:]).then_inc(s_fv, 1)
                        dve.wait_ge(s_fv, done + w * 3 + 4)
                        apart(dve)
                        base = dve.value_load(far_col_i[0:1, 0:1], min_val=0, max_val=N)
                        here = agg[:, bass.ds(base, WIN)]
                        dve.wait_ge(s_fmm, m + 1)
                        nc.vector.tensor_tensor(here, here, p_agg, ALU.add).then_inc(s_fadd, 1)
                        dve.wait_ge(s_fadd, m + 1)
                        apart(dve)

            def onehots(buf, rel):
                return nc.vector.tensor_tensor(
                    buf[:], col[:].unsqueeze(1).to_broadcast([P, TILES, WIN]),
                    rel.unsqueeze(2).to_broadcast([P, TILES, WIN]), ALU.is_equal)

            def products(buf, features):
                xj = buf[:, :, 0:D].unsqueeze(2).to_broadcast([P, TILES, F, D])
                ef = features[:].unsqueeze(3).to_broadcast([P, TILES, F, D])
                return nc.vector.tensor_tensor(
                    buf[:, :, D:D + FD].rearrange("p j (f d) -> p j f d", d=D), xj, ef, ALU.mult)

            def segments(layer):
                with dve.Fori(0, BODIES) as b:
                    first = layer * G + b * SLOTS

                    def add(u):
                        base = dve.value_load(base_i[0:1, bass.ds(b * SLOTS + u, 1)], min_val=0, max_val=N - 1)
                        here = agg[:, bass.ds(base, WIN)]
                        dve.wait_ge(s_mm, first + (u + 1))
                        dve.wait_ge(s_add, first + (u + CREDIT))
                        nc.vector.tensor_tensor(here, here, p_agg, ALU.add).then_inc(s_add, 1)

                    for u in range(SLOTS):
                        dve.wait_ge(s_seg, first + (u + CREDIT - 1))
                        rel = dst_rel[:, bass.ds(b * SLOTS + u, 1), :].rearrange("p g j -> p (g j)")
                        onehots(hot[u % HOTS], rel).then_inc(s_hot, 1)
                        if u:
                            add(u - 1)
                        dve.wait_ge(s_idx[u], (layer * BODIES + b) * 32 + 32)
                        dve.wait_ge(s_gath[u], (layer * BODIES + b) * (16 * TILES) + 16 * TILES)
                        products(xp[u], ea[u]).then_inc(s_prod, 1)
                    add(SLOTS - 1)
                dve.wait_ge(s_add, layer * G + (G + CREDIT))
                apart(dve)
                with dve.If(far > WIN - 1):
                    segments_far(layer)
                dve.sem_inc(s_mark, 1)

            set_weights(0)
            for c, u, n in node_chunks(dve, 0):
                dve.wait_ge(s_root, n + (1 + CREDIT))
                root_sum(0, c, u % HOTS)
            dve.wait_ge(s_node, CHUNKS + CREDIT)

            BN_STEPS = 4
            with dve.Fori(0, L - 1) as layer:
                segments(layer)
                taken = [0]

                def link(ins):
                    taken[0] += 1
                    ins.then_inc(s_v, 1)
                    dve.wait_ge(s_v, layer * BN_STEPS + (steps[0] + taken[0]))

                with dve.Fori(0, CHUNKS) as c:
                    nc.vector.bn_stats(bn_s[:, bass.ds(c, 1), :].rearrange("d c s -> d (c s)"),
                                       agg[:, bass.ds(c * CN, CN)]).then_inc(s_stats, 1)
                dve.wait_ge(s_stats, layer * CHUNKS + CHUNKS)
                apart(dve)
                nc.vector.bn_aggr(bn_m[:], bn_s[:].rearrange("d c s -> d (c s)")).then_inc(s_var, 1)
                dve.wait_ge(s_std, layer + 2)
                link(nc.vector.reciprocal(bn_r[:], bn_d[:]))
                link(nc.vector.tensor_tensor(bn_a[:], bn_r[:], gam[:, bass.ds(layer, 1)], ALU.mult))
                link(nc.vector.tensor_tensor(bn_t[:], bn_m[:, 0:1], bn_a[:], ALU.mult))
                link(nc.vector.tensor_tensor(bn_b[:], bet[:, bass.ds(layer, 1)], bn_t[:], ALU.subtract))
                assert taken[0] == BN_STEPS
                dve.sem_inc(s_bn, 1)
                set_weights(layer + 1)
                for c, u, n in node_chunks(dve, (layer + 1) * CHUNKS):
                    dve.wait_ge(s_root, n + (1 + CREDIT))
                    nc.vector.tensor_copy(rows[:, bass.ds(c * SUB, SUB), :], p_t[u % HOTS])
                    root_sum(layer + 1, c, u % HOTS)
                dve.wait_ge(s_node, (layer + 2) * CHUNKS + CREDIT)
                dve.sem_inc(s_rows, 1)
            segments(L - 1)
            dve.sem_inc(s_bn, 1)
            for c, u, n in node_chunks(dve, L * CHUNKS):
                dve.wait_ge(s_root, n + (1 + CREDIT))
                nc.vector.tensor_tensor(rows[:, bass.ds(c * SUB, SUB), :], p_t[u % HOTS],
                                        x_nm[:, bass.ds(c * SUB, SUB), :], ALU.add).then_inc(s_node, 1)
            dve.wait_ge(s_node, (L + 1) * CHUNKS + CREDIT)
            nc.vector.tensor_tensor(rows[:], rows[:], pb[:].unsqueeze(1).to_broadcast([NODE_P, PER, D]),
                                    ALU.add).then_inc(s_rows, 1)

        @block.scalar
        def _(act):
            act.wait_ge(s_var, 1)
            nc.scalar.activation(ln_v[:], ln_v[:], ACT.Sqrt, bias=eps[0:NODE_P, :], scale=1.0 / D).then_inc(s_std, 1)
            act.wait_ge(s_rows, 1)
            for c, u, n in node_chunks(act, 0):
                act.wait_ge(s_root, n + 1)
                nc.scalar.activation(stage[u][:], rows[:, bass.ds(c * SUB, SUB), :], ACT.Copy).then_inc(s_stage, 1)
                act.wait_ge(s_chT, n + 1)
                nc.scalar.activation(hT[u][:], p_h, ACT.Copy).then_inc(s_hT, 1)

            far = farthest(act)

            def copy_segments_far(layer):
                with act.Fori(0, G) as g:
                    with act.Fori(0, FAR) as w:
                        act.wait_ge(s_fseg, (layer * G + g) * FAR + w + 1)
                        nc.scalar.activation(zT[:], p_z, ACT.Copy)
                        nc.scalar.activation(zxT[:], p_zx, ACT.Copy).then_inc(s_fzT, 1)

            def copy_segments(layer):
                with act.Fori(0, BODIES) as b:
                    for u in range(SLOTS):
                        k = layer * G + b * SLOTS + u
                        act.wait_ge(s_seg, k + (1 + CREDIT))
                        nc.scalar.activation(zT[:], p_z, ACT.Copy)
                        nc.scalar.activation(zxT[:], p_zx, ACT.Copy).then_inc(s_zT, 1)
                with act.If(far > WIN - 1):
                    copy_segments_far(layer)
                act.sem_inc(s_mark, 1)

            with act.Fori(0, L - 1) as layer:
                copy_segments(layer)
                act.wait_ge(s_var, layer + 2)
                nc.scalar.activation(bn_d[:], bn_m[:, 1:2], ACT.Sqrt, bias=eps[0:D, :]).then_inc(s_std, 1)
                act.wait_ge(s_bn, layer + 1)
                for c, u, n in node_chunks(act, (layer + 1) * CHUNKS):
                    act.wait_ge(s_root, n + 1)
                    nc.scalar.activation(hT[u][:], chunk_of(c), ACT.Relu, bias=bn_b[:], scale=bn_a[:]).then_inc(s_hT, 1)
            copy_segments(L - 1)
            act.wait_ge(s_bn, L)
            for c, u, n in node_chunks(act, L * CHUNKS):
                act.wait_ge(s_root, n + 1)
                nc.scalar.activation(hT[u][:], chunk_of(c), ACT.Relu).then_inc(s_hT, 1)

        @block.tensor
        def _(pe):
            for _ in range(CREDIT):
                pe.sem_inc(s_root, 1)
                pe.sem_inc(s_seg, 1)
            pe.wait_ge(s_ident, 1)
            pe.wait_ge(s_w, 1)
            for c, u, n in node_chunks(pe, 0):
                pe.wait_ge(s_stage, n + 1)
                for m in range(SUB):
                    last = nc.tensor.transpose(p_h[:, m, :], stage[u][:, m, :], ident[0:NODE_P, 0:NODE_P])
                last.then_inc(s_chT, 1)
                pe.wait_ge(s_hT, n + 1)
                pe.wait_ge(s_node, n + (CREDIT - 1))
                apart(pe)
                nc.tensor.matmul(p_r[u % HOTS], rw_now[:], hT[u][:], start=True, stop=True).then_inc(s_root, 1)

            far = farthest(pe)

            def sum_tiles(products, onehots):
                for j in range(TILES):
                    ends = dict(start=j == 0, stop=j == TILES - 1)
                    nc.tensor.matmul(p_z, products[:, j, D:D + FD], onehots[:, j, :], **ends)
                    last = nc.tensor.matmul(p_zx, products[:, j, 0:D], onehots[:, j, :], **ends)
                return last

            def messages():
                nc.tensor.matmul(p_agg, w_now[:], zT[:], start=True, stop=False)
                return nc.tensor.matmul(p_agg, eb_now[:], zxT[:], start=False, stop=True)

            def segment_sums_far(layer):
                with pe.Fori(0, G) as g:
                    pe.wait_ge(s_fprod, layer * G + g + 1)
                    apart(pe)
                    with pe.Fori(0, FAR) as w:
                        m = (layer * G + g) * FAR + w
                        pe.wait_ge(s_fhot, m + 1)
                        sum_tiles(xp[0], hot[0]).then_inc(s_fseg, 1)
                        pe.wait_ge(s_fzT, m + 1)
                        messages().then_inc(s_fmm, 1)

            def segment_sums(layer):
                with pe.Fori(0, BODIES) as b:
                    for u in range(SLOTS):
                        k = layer * G + b * SLOTS + u
                        pe.wait_ge(s_hot, k + 1)
                        pe.wait_ge(s_prod, k + (1 + CREDIT))
                        sum_tiles(xp[u], hot[u % HOTS]).then_inc(s_seg, 1)
                        pe.wait_ge(s_zT, k + 1)
                        pe.wait_ge(s_add, k + CREDIT)
                        messages().then_inc(s_mm, 1)
                with pe.If(far > WIN - 1):
                    segment_sums_far(layer)
                pe.sem_inc(s_mark, 1)

            with pe.Fori(0, L - 1) as layer:
                segment_sums(layer)
                pe.wait_ge(s_w, layer + 2)
                apart(pe)
                for c, u, n in node_chunks(pe, (layer + 1) * CHUNKS):
                    pe.wait_ge(s_hT, n + 1)
                    pe.wait_ge(s_node, n + (CREDIT - 1))
                    apart(pe)
                    for m in range(SUB):
                        nc.tensor.transpose(p_t[u % HOTS][:, m, :], hT[u][:, m, :], ident[0:D, 0:D])
                    nc.tensor.matmul(p_r[u % HOTS], rw_now[:], hT[u][:], start=True, stop=True).then_inc(s_root, 1)
            segment_sums(L - 1)
            for c, u, n in node_chunks(pe, L * CHUNKS):
                pe.wait_ge(s_hT, n + 1)
                pe.wait_ge(s_node, n + (CREDIT - 1))
                apart(pe)
                for m in range(SUB):
                    last = nc.tensor.matmul(p_t[u % HOTS][:, m, :], hT[u][:, m, :], pw[:], start=True, stop=True)
                last.then_inc(s_root, 1)


def kernel(**inputs):
    import numpy as _np
    import concourse.bacc as _bacc
    from concourse import mybir as _mybir
    from concourse.bass_utils import run_bass_kernel_spmd as _run

    w = {k.removeprefix("L0_gnn_"): _np.asarray(v) for k, v in inputs.items()}
    laid = {
        "x": w["x"], "src": w["src"], "dst": w["dst"], "edge_attr": w["edge_attr_8"],
        "edge_w": w["edge_w"], "edge_b": w["edge_b"], "root_w": w["root_w"],
        "root_b": w["root_b"].T, "gamma": w["bn_gamma"].T, "beta": w["bn_beta"].T,
        "pred_w": w["pred_w"], "pred_b": w["pred_b"],
    }
    nc = _bacc.Bacc("TRN2", target_bir_lowering=False, num_devices=1)
    arrays, args = {}, []
    for name, a in laid.items():
        a = _np.ascontiguousarray(a)
        arrays[f"in_{name}"] = a
        args.append(nc.dram_tensor(f"in_{name}", a.shape, _mybir.dt.from_np(a.dtype), kind="ExternalInput").ap())
    o = nc.dram_tensor("out_x", w["x"].shape, _mybir.dt.float32, kind="ExternalOutput").ap()
    gnn_kernel(nc, *args, o)
    r = _run(nc, [arrays], core_ids=[0])
    return r.results[0]["out_x"]
```

```python
from contextlib import ExitStack

import concourse.bass as bass
from concourse import mybir

P = 128
ALU = mybir.AluOpType
ACT = mybir.ActivationFunctionType
AX_X = mybir.AxisListType.X
F32 = mybir.dt.float32
F32R = mybir.dt.float32r
I16 = mybir.dt.int16
I32 = mybir.dt.int32
RMAX = bass.bass_isa.ReduceOp.max

TILES = 25
PICKED = 8
FETCHED = TILES - PICKED
FOLD = 4
FOLD_BITS = 2
BANKS = 4
SLOTS = 5
PAIR = 2
HALF = PICKED // 2
KEYS = 3
TURNS = 3
WIN = 112
NODE_P = 125
SUB = 4
LN_EPS = 1e-5
BN_EPS = 1e-5
CREDIT = SLOTS


def gnn_kernel(nc, x, src, dst, edge_attr, edge_w, edge_b, root_w, root_b, gamma, beta, pred_w, pred_b, out):
    N, D = x.shape
    E, F = edge_attr.shape
    L = edge_w.shape[0]
    FD = F * D
    GE = P * TILES
    G = E // GE
    BODIES = G // SLOTS
    PER = N // NODE_P
    CHUNKS = PER // SUB
    CN = NODE_P * SUB
    WINDOWS = -(-N // WIN)
    assert E == G * GE and G == BODIES * SLOTS and FD == P and D * (F + 1) <= 512
    assert N == NODE_P * PER and PER == CHUNKS * SUB and CHUNKS % SLOTS == 0 and CN <= 512

    FINE = -(-N // (P * FOLD))
    SELW = FINE * D
    assert SELW <= 512

    table = nc.dram_tensor("node_table", [N, D], F32, kind="Internal").ap()
    keys = nc.dram_tensor("edge_keys", [G * PICKED, P], I16, kind="Internal").ap()

    def parts(a, tail=""):
        v = a.rearrange(f"(g e) {tail} -> g e {tail}", g=G)
        return [w.rearrange(f"g (p j) {tail} -> g p j {tail}", p=P)
                for w in (v[:, 0:P * FETCHED], v[:, P * FETCHED:GE])]

    src_f, src_p = parts(src)
    dst_f, dst_p = parts(dst)
    ea_f, ea_p = parts(edge_attr, "f")
    cols_f, cols_p = slice(0, FETCHED), slice(FETCHED, TILES)

    with ExitStack() as ctx:
        def sb(name, shape, dt=F32):
            return ctx.enter_context(nc.sbuf_tensor(name, shape, dt))

        def ps(name, shape):
            return ctx.enter_context(nc.psum_tensor(name, shape, F32))

        def sem(name):
            return ctx.enter_context(nc.semaphore(name))

        idx = [sb(f"idx{u}", [P, FETCHED], I32) for u in range(SLOTS)]
        ea = [sb(f"ea{u}", [P, TILES, F]) for u in range(SLOTS)]
        xp = [sb(f"xp{i}", [P, TILES, D + FD]) for i in range(PAIR)]
        hot = [sb(f"hot{i}", [P, TILES, WIN]) for i in range(PAIR)]
        xg = [sb(f"xg{u}", [P, TILES, D]) for u in range(SLOTS)]
        key = [sb(f"key{i}", [P, PICKED, P], I16) for i in range(KEYS)]
        low_hot = sb("low_hot", [P, FOLD, PICKED, P], F32R)
        low_id = sb("low_id", [P, FOLD])
        distance = [sb(f"distance{i}", [P, HALF, P], mybir.dt.bfloat16) for i in range(FOLD)]
        one = sb("one", [P, 1])
        fine = sb("fine", [P, G * PICKED])
        spread = sb("spread", [P, HALF, D, FINE])
        nodes = [sb(f"nodes{i}", [P, FOLD, FINE, D], F32R) for i in range(2)]
        nodes_raw, nodes_cut = (t[:].rearrange("p a b -> p (a b)")[:, 0:FOLD * SELW]
                                .rearrange("p (k f d) -> p k f d", k=FOLD, d=D) for t in (xp[0], hot[0]))
        dst_rel = sb("dst_rel", [P, G, TILES])
        base_i = sb("base_i", [P, G], I32)
        far_i = sb("far_i", [P, 1], I32)
        scratch = xp[1][:].rearrange("p a b -> p (a b)")
        GP = G * PICKED
        assert PICKED == 2 * HALF and FOLD == 1 << FOLD_BITS and 3 * GP + PICKED * P // 2 <= TILES * (D + FD) and G <= P
        src_pick = scratch[:, 0:GP].bitcast(I32).rearrange("p (g j) -> p g j", g=G)
        src_int = scratch[:, GP:2 * GP].bitcast(I32).rearrange("p (g j) -> p g j", g=G)
        key_f = scratch[:, 2 * GP:3 * GP].rearrange("p (g j) -> p g j", g=G)
        key16 = scratch[0:G, 3 * GP:3 * GP + PICKED * P // 2].bitcast(I16).rearrange("q (c p) -> q c p", p=P)
        agg = sb("agg", [D, N + WIN])
        rows = sb("rows", [NODE_P, PER, D])
        x_nm = hot[1][0:NODE_P, :, :].rearrange("p a b -> p (a b)")[:, 0:PER * D].rearrange("p (m d) -> p m d", d=D)
        stage = [sb(f"stage{u}", [NODE_P, SUB, D]) for u in range(SLOTS)]
        hT = [sb(f"hT{u}", [D, SUB, NODE_P]) for u in range(SLOTS)]
        w_all = sb("w_all", [P, L, D])
        eb_all = sb("eb_all", [D, L, D])
        rw_all = sb("rw_all", [D, L, D])
        rb_all = sb("rb_all", [D, L])
        w_now = sb("w_now", [P, D])
        eb_now = sb("eb_now", [D, D])
        rw_now = sb("rw_now", [D, D])
        gam = sb("gam", [D, L - 1])
        bet = sb("bet", [D, L - 1])
        pw = sb("pw", [D, D])
        pb = sb("pb", [NODE_P, D])
        col_i = sb("col_i", [P, P], I32)
        row_i = sb("row_i", [P, 1], I32)
        low_id_i = sb("low_id_i", [P, FOLD], I32)
        col = sb("col", [P, P])
        row = sb("row", [P, 1])
        ident = sb("ident", [P, P])
        eps = sb("eps", [P, 1])
        z = sb("z", [WIN, D + FD])
        zT = sb("zT", [P, WIN])
        zxT = sb("zxT", [D, WIN])
        low_p = sb("low_p", [P, G])
        low_a = sb("low_a", [P, G])
        far_p = sb("far_p", [P, 1])
        far_a = sb("far_a", [P, 1])
        ln_m = sb("ln_m", [NODE_P, PER])
        ln_v = sb("ln_v", [NODE_P, PER])
        ln_r = sb("ln_r", [NODE_P, PER])
        bn_s = sb("bn_s", [D, CHUNKS, 6])
        bn_m = sb("bn_m", [D, 2])
        bn_d = sb("bn_d", [D, 1])
        bn_r = sb("bn_r", [D, 1])
        bn_a = sb("bn_a", [D, 1])
        bn_t = sb("bn_t", [D, 1])
        bn_b = sb("bn_b", [D, 1])
        far_idx = sb("far_idx", [P, TILES], I32)
        far_ea = sb("far_ea", [P, TILES, F])
        far_rel = sb("far_rel", [P, TILES])
        far_col = sb("far_col", [P, 1])
        far_col_i = sb("far_col_i", [P, 1], I32)

        bank = [ps(f"bank{i}", [P, 512]) for i in range(8)]
        p_z, p_agg = bank[0][0:WIN, 0:D + FD], bank[2][0:D, 0:WIN]
        p_zT, p_zxT = bank[1][:, 0:WIN], bank[1][0:D, WIN:2 * WIN]
        p_sel = [bank[3 + i][:, 0:SELW] for i in range(BANKS)]
        p_t = [bank[i][0:NODE_P, 0:SUB * D].rearrange("p (m d) -> p m d", d=D) for i in range(TURNS)]
        p_h, *p_r = [bank[i][0:D, 0:CN].rearrange("d (m p) -> d m p", m=SUB) for i in range(TURNS, 2 * TURNS + 1)]

        s_const = sem("const_loaded")
        s_dst = sem("dst_loaded")
        s_iota = sem("iota_done")
        s_v = sem("vector_step")
        s_base = sem("base_ready")
        s_baseall = sem("base_reduced")
        s_far = sem("far_ready")
        s_farall = sem("far_reduced")
        s_flag = sem("flag_ready")
        s_ident = sem("ident_ready")
        s_var = sem("variance_ready")
        s_std = sem("std_ready")
        s_rows = sem("rows_ready")
        s_table = sem("table_written")
        s_w = sem("weights_set")
        s_stats = sem("chunk_stats")
        s_bn = sem("norm_ready")
        s_stage = sem("chunk_staged")
        s_chT = sem("chunk_transposed")
        s_hT = sem("chunk_normed")
        s_root = sem("chunk_products")
        s_node = sem("chunk_done")
        s_idx = [sem(f"edges_loaded{u}") for u in range(SLOTS)]
        s_gath = [sem(f"gathered{u}") for u in range(SLOTS)]
        s_src = sem("picked_sources_loaded")
        s_keyf = sem("keys_in_float")
        s_keyT = sem("keys_transposed")
        s_key16 = sem("keys_in_int16")
        s_keyd = sem("keys_written")
        s_key = [sem(f"keys_loaded{u}") for u in range(SLOTS)]
        s_nload = sem("nodes_loaded")
        s_tail = sem("tail_cleared")
        s_split = sem("upper_parts_ready")
        s_nodes = sem("nodes_split")
        s_dist = sem("distances_ready")
        s_low = sem("low_onehot_ready")
        s_pick = sem("tile_picked")
        s_taken = sem("pick_taken")
        s_xg = sem("picks_summed")
        s_xc = sem("rows_copied")
        s_hot = sem("onehot_ready")
        s_prod = sem("products_ready")
        s_seg = sem("segments_summed")
        s_z = sem("sums_copied")
        s_T = sem("sums_transposed")
        s_zT = sem("transposed_copied")
        s_mm = sem("messages_ready")
        s_add = sem("messages_added")
        s_x = sem("x_loaded_again")
        s_out = sem("output_written")
        s_mark = sem("wait_passed")
        s_fgo = sem("far_group_begun")
        s_fload = sem("far_edges_loaded")
        s_fgath = sem("far_gathered")
        s_fprod = sem("far_products_ready")
        s_fv = sem("far_vector_step")
        s_fhot = sem("far_onehot_ready")
        s_fseg = sem("far_segments_summed")
        s_fz = sem("far_sums_copied")
        s_fT = sem("far_sums_transposed")
        s_fzT = sem("far_transposed_copied")
        s_fmm = sem("far_messages_ready")
        s_fadd = sem("far_messages_added")

        block = ctx.enter_context(nc.Block())

        def chunk_of(c):
            return agg[:, 0:N].rearrange("d (p m) -> d m p", m=PER)[:, bass.ds(c * SUB, SUB), :]

        def bodies(eng):
            yield 0, True, False
            with eng.Fori(1, BODIES - 1) as b:
                yield b, False, False
            yield BODIES - 1, False, True

        def node_chunks(eng, n0):
            with eng.Fori(0, CHUNKS // SLOTS) as cb:
                for u in range(SLOTS):
                    yield cb * SLOTS + u, u, n0 + cb * SLOTS + u

        def apart(eng):
            eng.sem_inc(s_mark, 1)

        FAR = WINDOWS - 1

        def farthest(eng):
            eng.wait_ge(s_flag, 1)
            return eng.value_load(far_i[0:1, 0:1], min_val=0, max_val=N)

        @block.sync
        def _(sp):
            sp.dma_start(src_pick, src_p.rearrange("g p j -> p g j")).then_inc(s_src, 16)
            dst_i = dst_rel[:].bitcast(I32)
            sp.dma_start(dst_i[:, :, cols_f], dst_f.rearrange("g p j -> p g j")).then_inc(s_dst, 16)
            sp.dma_start(dst_i[:, :, cols_p], dst_p.rearrange("g p j -> p g j")).then_inc(s_dst, 16)
            sp.dma_start(x_nm, x.rearrange("(p m) d -> p m d", m=PER)).then_inc(s_const, 16)
            sp.dma_start(w_all[:], edge_w.rearrange("l f (i o) -> (f i) l o", o=D)).then_inc(s_const, 16)
            sp.dma_start(eb_all[:], edge_b.rearrange("l (i o) -> i l o", o=D)).then_inc(s_const, 16)
            sp.dma_start(rw_all[:], root_w.rearrange("l i o -> i l o")).then_inc(s_const, 16)
            sp.dma_start(rb_all[:], root_b).then_inc(s_const, 16)
            sp.dma_start(gam[:], gamma).then_inc(s_const, 16)
            sp.dma_start(bet[:], beta).then_inc(s_const, 16)
            sp.dma_start(pw[:], pred_w).then_inc(s_const, 16)
            sp.dma_start(pb[:], pred_b[None, :].to_broadcast([NODE_P, D])).then_inc(s_const, 16)

            def write_table():
                sp.dma_start(table.rearrange("(p m) d -> p m d", m=PER), rows[:]).then_inc(s_table, 16)

            def load_nodes():
                whole = N // P
                by_block = table[0:whole * P, :].rearrange("(m p) d -> p m d", p=P)
                for k in range(FOLD):
                    count = len(range(k, whole, FOLD))
                    sp.dma_start(nodes_raw[:, k, 0:count, :], by_block[:, k::FOLD, :]).then_inc(s_nload, 16)
                sp.dma_start(nodes_raw[0:N - whole * P, whole % FOLD, whole // FOLD, :],
                             table[whole * P:N, :]).then_inc(s_nload, 16)

            sp.wait_ge(s_key16, PICKED)
            sp.dma_start(keys.rearrange("(c q) p -> q c p", q=G), key16).then_inc(s_keyd, 16)
            sp.wait_ge(s_rows, 1)
            write_table()
            sp.wait_ge(s_table, 16)
            sp.wait_ge(s_tail, 1)
            load_nodes()
            sp.wait_ge(s_keyd, 16)

            far = farthest(sp)

            def load_far(layer):
                with sp.Fori(0, G) as g:
                    n = layer * G + g
                    sp.wait_ge(s_fgo, n + 1)
                    for cols, of_src, of_ea in ((cols_f, src_f, ea_f), (cols_p, src_p, ea_p)):
                        sp.dma_start(far_idx[:, cols], of_src[bass.ds(g, 1), :, :]
                                     .rearrange("g p j -> (g p) j")).then_inc(s_fload, 16)
                        sp.dma_start(far_ea[:, cols, :], of_ea[bass.ds(g, 1), :, :, :]
                                     .rearrange("g p j f -> (g p) j f")).then_inc(s_fload, 16)

            def load_edges(layer):
                with sp.Fori(0, BODIES) as b:
                    for u in range(SLOTS):
                        sp.wait_ge(s_prod, layer * G + b * SLOTS + (u + 1))
                        g = bass.ds(b * SLOTS + u, 1)
                        sp.dma_start(idx[u][:], src_f[g, :, :].rearrange("g p j -> (g p) j")).then_inc(s_idx[u], 16)
                        sp.dma_start(ea[u][:, cols_f, :], ea_f[g, :, :, :]
                                     .rearrange("g p j f -> (g p) j f")).then_inc(s_idx[u], 16)
                        sp.dma_start(ea[u][:, cols_p, :], ea_p[g, :, :, :]
                                     .rearrange("g p j f -> (g p) j f")).then_inc(s_idx[u], 16)
                        sp.wait_ge(s_keyd, 16)
                        sp.wait_ge(s_low, (layer * G + b * SLOTS) * 2 + (2 * u + 2 * CREDIT - 2))
                        sp.dma_start(
                            key[u % KEYS][:].rearrange("p t e -> p (t e)"),
                            keys[bass.ds((b * SLOTS + u) * PICKED, PICKED), :].rearrange("(a t) e -> a (t e)", a=1)
                            .to_broadcast([P, PICKED * P])).then_inc(s_key[u], 16)
                with sp.If(far > WIN - 1):
                    load_far(layer)
                sp.sem_inc(s_mark, 1)

            with sp.Fori(0, L - 1) as layer:
                load_edges(layer)
                sp.wait_ge(s_rows, layer + 2)
                write_table()
                sp.wait_ge(s_table, layer * 16 + 32)
                sp.wait_ge(s_tail, layer + 2)
                load_nodes()
            load_edges(L - 1)
            sp.wait_ge(s_bn, L)
            sp.dma_start(x_nm, x.rearrange("(p m) d -> p m d", m=PER)).then_inc(s_x, 16)
            sp.wait_ge(s_rows, L + 1)
            sp.dma_start(out.rearrange("(p m) d -> p m d", m=PER), rows[:]).then_inc(s_out, 16)
            sp.wait_ge(s_out, 16)

        @block.gpsimd
        def _(pool):
            pool.iota(col_i[:], [[1, P]], base=0, channel_multiplier=0).then_inc(s_iota, 1)
            pool.iota(row_i[:], [[0, 1]], base=0, channel_multiplier=1).then_inc(s_iota, 1)
            for k in range(FOLD):
                pool.iota(low_id_i[:, k:k + 1], [[0, 1]], base=k * P, channel_multiplier=1).then_inc(s_iota, 1)
            pool.wait_ge(s_base, 1)
            pool.partition_all_reduce(low_a[:], low_p[:], P, RMAX).then_inc(s_baseall, 1)
            pool.wait_ge(s_far, 1)
            pool.partition_all_reduce(far_a[:], far_p[:], P, RMAX).then_inc(s_farall, 1)

            far = farthest(pool)

            def gather_far(layer):
                with pool.Fori(0, G) as g:
                    pool.wait_ge(s_fload, (layer * G + g) * 64 + 64)
                    apart(pool)
                    for j in range(TILES):
                        pool.indirect_dma_start(
                            out=xp[0][:, j, 0:D], out_offset=None, in_=table[:, :],
                            in_offset=bass.IndirectOffsetOnAxis(ap=far_idx[:, j:j + 1], axis=0),
                        ).then_inc(s_fgath, 16)

            def gather(layer):
                pool.wait_ge(s_table, layer * 16 + 16)
                apart(pool)
                with pool.Fori(0, BODIES) as b:
                    for u in range(SLOTS):
                        pool.wait_ge(s_idx[u], (layer * BODIES + b) * 48 + 48)
                        pool.wait_ge(s_seg, layer * G + b * SLOTS + (u + 1))
                        apart(pool)
                        for j in range(FETCHED):
                            pool.indirect_dma_start(
                                out=xg[u][:, j, :], out_offset=None, in_=table[:, :],
                                in_offset=bass.IndirectOffsetOnAxis(ap=idx[u][:, j:j + 1], axis=0),
                            ).then_inc(s_gath[u], 16)
                with pool.If(far > WIN - 1):
                    gather_far(layer)
                pool.sem_inc(s_mark, 1)

            with pool.Fori(0, L - 1) as layer:
                gather(layer)
            gather(L - 1)

        @block.vector
        def _(dve):
            steps = [0]

            def step(ins):
                steps[0] += 1
                ins.then_inc(s_v, 1)
                dve.wait_ge(s_v, steps[0])

            dve.sem_inc(s_xg, 1)
            dve.sem_inc(s_dist, 1)
            for _ in range(2 * CREDIT):
                dve.sem_inc(s_low, 1)
            for _ in range(PICKED):
                dve.sem_inc(s_taken, 1)
            def clear_tail():
                nc.vector.memset(nodes_raw[:, :, N // (P * FOLD):FINE, :], 0.0).then_inc(s_tail, 1)

            for _ in range(CREDIT):
                dve.sem_inc(s_prod, 1)
                dve.sem_inc(s_add, 1)
                dve.sem_inc(s_node, 1)
            dve.wait_ge(s_iota, 2 + FOLD)
            nc.vector.tensor_scalar(low_id[:], low_id_i[:], -1.0, None, ALU.mult)
            nc.vector.memset(one[:], 1.0)
            nc.vector.tensor_copy(col[:], col_i[:])
            nc.vector.memset(eps[:], LN_EPS)
            nc.vector.memset(agg[:, N:N + WIN], 0.0)
            step(nc.vector.tensor_copy(row[:], row_i[:]))
            nc.vector.tensor_scalar(ident[:], col[:], row[:, 0:1], None, ALU.is_equal).then_inc(s_ident, 1)

            dve.wait_ge(s_src, 16)
            step(nc.vector.tensor_scalar(src_int, src_pick, 7 + FOLD_BITS, None, ALU.logical_shift_right))
            step(nc.vector.tensor_copy(fine[:].rearrange("p (g j) -> p g j", g=G), src_int))
            step(nc.vector.tensor_scalar(src_int, src_pick, P * FOLD - 1, None, ALU.bitwise_and))
            nc.vector.tensor_copy(key_f, src_int).then_inc(s_keyf, 1)
            for c in range(PICKED):
                dve.wait_ge(s_keyT, c + 1)
                nc.vector.tensor_copy(key16[:, c, :], bank[c % 2][0:G, 0:P]).then_inc(s_key16, 1)

            dve.wait_ge(s_const, 9 * 16)
            step(nc.vector.tensor_reduce(ln_m[:], x_nm, AX_X, ALU.add))
            step(nc.vector.tensor_scalar(ln_m[:], ln_m[:], 1.0 / D, None, ALU.mult))
            ln_mb = ln_m[:].unsqueeze(2).to_broadcast([NODE_P, PER, D])
            step(nc.vector.tensor_tensor(rows[:], x_nm, ln_mb, ALU.subtract))
            squares = hot[0][0:NODE_P, :, :].rearrange("p a b -> p (a b)")[:, 0:PER * D].rearrange("p (m d) -> p m d", d=D)
            step(nc.vector.tensor_tensor(squares, rows[:], rows[:], ALU.mult))
            nc.vector.tensor_reduce(ln_v[:], squares, AX_X, ALU.add).then_inc(s_var, 1)
            dve.wait_ge(s_std, 1)
            step(nc.vector.reciprocal(ln_r[:], ln_v[:]))
            ln_rb = ln_r[:].unsqueeze(2).to_broadcast([NODE_P, PER, D])
            step(nc.vector.tensor_tensor(rows[:], rows[:], ln_rb, ALU.mult))
            clear_tail()
            nc.vector.tensor_scalar(rows[:], rows[:], 0.0, None, ALU.max).then_inc(s_rows, 1)

            dve.wait_ge(s_dst, 32)
            step(nc.vector.tensor_copy(dst_rel[:], dst_rel[:].bitcast(I32)))
            step(nc.vector.tensor_reduce(low_p[:], dst_rel[:], AX_X, ALU.min))
            nc.vector.tensor_scalar(low_p[:], low_p[:], -1.0, None, ALU.mult).then_inc(s_base, 1)
            dve.wait_ge(s_baseall, 1)
            step(nc.vector.tensor_scalar(low_a[:], low_a[:], -1.0, None, ALU.mult))
            step(nc.vector.tensor_copy(base_i[:], low_a[:]))
            low_b = low_a[:].unsqueeze(2).to_broadcast([P, G, TILES])
            step(nc.vector.tensor_tensor(dst_rel[:], dst_rel[:], low_b, ALU.subtract))
            nc.vector.tensor_reduce(far_p[:], dst_rel[:].rearrange("p g j -> p (g j)"), AX_X,
                                    ALU.max).then_inc(s_far, 1)
            dve.wait_ge(s_farall, 1)
            step(nc.vector.tensor_copy(far_i[:], far_a[:]))
            dve.sem_inc(s_flag, 1)
            far = farthest(dve)

            def set_weights(layer):
                nc.vector.tensor_copy(w_now[:], w_all[:, bass.ds(layer, 1), :].rearrange("p l o -> p (l o)"))
                nc.vector.tensor_copy(eb_now[:], eb_all[:, bass.ds(layer, 1), :].rearrange("p l o -> p (l o)"))
                nc.vector.tensor_copy(rw_now[:], rw_all[:, bass.ds(layer, 1), :].rearrange("p l o -> p (l o)")
                                      ).then_inc(s_w, 1)

            def root_sum(layer, c, i):
                nc.vector.tensor_scalar(chunk_of(c), p_r[i], rb_all[:, bass.ds(layer, 1)], None,
                                        ALU.add).then_inc(s_node, 1)

            def segments_far(layer):
                with dve.Fori(0, G) as g:
                    n = layer * G + g
                    done = n * (1 + 3 * FAR)
                    dve.sem_inc(s_fgo, 1)
                    nc.vector.tensor_copy(far_rel[:], dst_rel[:, bass.ds(g, 1), :].rearrange("p g j -> p (g j)"))
                    nc.vector.tensor_copy(far_col[:], low_a[:, bass.ds(g, 1)]).then_inc(s_fv, 1)
                    dve.wait_ge(s_fload, n * 64 + 64)
                    dve.wait_ge(s_fgath, n * (16 * TILES) + 16 * TILES)
                    products(xp[0], xp[0][:, :, 0:D], far_ea).then_inc(s_fprod, 1)
                    with dve.Fori(0, FAR) as w:
                        m = n * FAR + w
                        dve.wait_ge(s_fv, done + w * 3 + 1)
                        nc.vector.tensor_scalar(far_rel[:], far_rel[:], -float(WIN), None, ALU.add).then_inc(s_fv, 1)
                        nc.vector.tensor_scalar(far_col[:], far_col[:], float(WIN), float(N), ALU.add,
                                                ALU.min).then_inc(s_fv, 1)
                        dve.wait_ge(s_fv, done + w * 3 + 3)
                        onehots(hot[0], far_rel[:]).then_inc(s_fhot, 1)
                        nc.vector.tensor_copy(far_col_i[:], far_col[:]).then_inc(s_fv, 1)
                        dve.wait_ge(s_fv, done + w * 3 + 4)
                        apart(dve)
                        base = dve.value_load(far_col_i[0:1, 0:1], min_val=0, max_val=N)
                        here = agg[:, bass.ds(base, WIN)]
                        dve.wait_ge(s_fmm, m + 1)
                        nc.vector.tensor_tensor(here, here, p_agg, ALU.add).then_inc(s_fadd, 1)
                        dve.wait_ge(s_fadd, m + 1)
                        apart(dve)

            def onehots(buf, rel):
                return nc.vector.tensor_tensor(
                    buf[:], col[:, 0:WIN].unsqueeze(1).to_broadcast([P, TILES, WIN]),
                    rel.unsqueeze(2).to_broadcast([P, TILES, WIN]), ALU.is_equal)

            def products(buf, rows_of, features):
                xj = rows_of.unsqueeze(2).to_broadcast([P, TILES, F, D])
                ef = features[:].unsqueeze(3).to_broadcast([P, TILES, F, D])
                return nc.vector.tensor_tensor(
                    buf[:, :, D:D + FD].rearrange("p j (f d) -> p j f d", d=D), xj, ef, ALU.mult)

            def split_nodes(layer):
                dve.wait_ge(s_nload, (layer + 1) * (16 * (FOLD + 1)))
                nc.vector.tensor_scalar(nodes_cut.bitcast(I32), nodes_raw.bitcast(I32), -(1 << 12), None,
                                        ALU.bitwise_and).then_inc(s_split, 1)
                dve.wait_ge(s_split, layer + 1)
                nc.vector.tensor_copy(nodes[1][:], nodes_cut)
                nc.vector.tensor_tensor(nodes[0][:], nodes_raw, nodes_cut, ALU.subtract).then_inc(s_nodes, 1)
                dve.wait_ge(s_nodes, layer + 1)

            def compare_targets(layer, b, u):
                k = layer * G + b * SLOTS + u
                dve.wait_ge(s_seg, k + (CREDIT if u % SLOTS == 0 else CREDIT - 1))
                rel = dst_rel[:, bass.ds(b * SLOTS + u, 1), :].rearrange("p g j -> p (g j)")
                onehots(hot[u % SLOTS % PAIR], rel).then_inc(s_hot, 1)

            def take_picks(layer, b, u, half):
                k = layer * G + b * SLOTS + u
                t0, t1 = half * HALF, (half + 1) * HALF
                for t in range(t0, t1):
                    n = k * PICKED + t
                    dve.wait_ge(s_pick, n + (1 + PICKED))
                    if t == t0:
                        dve.wait_ge(s_xg, k * 2 + (half + 1))
                    nc.vector.scalar_tensor_tensor(
                        spread[:, t - t0, :, :].rearrange("p d f -> p f d"),
                        col[:, 0:FINE].unsqueeze(2).to_broadcast([P, FINE, D]),
                        fine[:, bass.ds((b * SLOTS + u) * PICKED + t, 1)],
                        p_sel[t % BANKS].rearrange("p (f d) -> p f d", d=D),
                        ALU.is_equal, ALU.mult).then_inc(s_taken, 1)
                dve.wait_ge(s_taken, k * PICKED + (t1 + PICKED))
                nc.vector.tensor_reduce(xg[u % SLOTS][:, FETCHED + t0:FETCHED + t1, :], spread[:, 0:t1 - t0, :, :],
                                        AX_X, ALU.add).then_inc(s_xg, 1)

            def multiply(layer, b, u):
                k = layer * G + b * SLOTS + u
                body = layer * BODIES + b
                dve.wait_ge(s_idx[u], body * 48 + 48)
                dve.wait_ge(s_gath[u], body * (16 * FETCHED) + 16 * FETCHED)
                dve.wait_ge(s_xg, k * 2 + 3)
                dve.wait_ge(s_seg, k + (CREDIT if u == 0 else CREDIT - 1))
                products(xp[u % PAIR], xg[u][:], ea[u]).then_inc(s_prod, 1)

            def add(layer, b, u):
                k = layer * G + b * SLOTS + u
                base = dve.value_load(base_i[0:1, bass.ds(b * SLOTS + u, 1)], min_val=0, max_val=N - 1)
                here = agg[:, bass.ds(base, WIN)]
                dve.wait_ge(s_mm, k + 1)
                dve.wait_ge(s_add, k + CREDIT)
                nc.vector.tensor_tensor(here, here, p_agg, ALU.add).then_inc(s_add, 1)

            def segments(layer):
                split_nodes(layer)
                compare_targets(layer, 0, 0)
                take_picks(layer, 0, 0, 0)
                take_picks(layer, 0, 0, 1)
                for b, first, last in bodies(dve):
                    for u in range(SLOTS):
                        another = not (last and u == SLOTS - 1)
                        early = (u + 1) % SLOTS != 0
                        multiply(layer, b, u)
                        if another:
                            take_picks(layer, b, u + 1, 0)
                            if early:
                                compare_targets(layer, b, u + 1)
                            take_picks(layer, b, u + 1, 1)
                        if not (first and u == 0):
                            add(layer, b, u - 1)
                        if another and not early:
                            compare_targets(layer, b, u + 1)
                add(layer, BODIES - 1, SLOTS - 1)
                dve.wait_ge(s_add, layer * G + (G + CREDIT))
                apart(dve)
                with dve.If(far > WIN - 1):
                    segments_far(layer)
                dve.sem_inc(s_mark, 1)

            set_weights(0)
            for c, u, n in node_chunks(dve, 0):
                dve.wait_ge(s_root, n + (1 + CREDIT))
                root_sum(0, c, u % TURNS)
            dve.wait_ge(s_node, CHUNKS + CREDIT)

            BN_STEPS = 4
            with dve.Fori(0, L - 1) as layer:
                segments(layer)
                taken = [0]

                def link(ins):
                    taken[0] += 1
                    ins.then_inc(s_v, 1)
                    dve.wait_ge(s_v, layer * BN_STEPS + (steps[0] + taken[0]))

                with dve.Fori(0, CHUNKS) as c:
                    nc.vector.bn_stats(bn_s[:, bass.ds(c, 1), :].rearrange("d c s -> d (c s)"),
                                       agg[:, bass.ds(c * CN, CN)]).then_inc(s_stats, 1)
                dve.wait_ge(s_stats, layer * CHUNKS + CHUNKS)
                apart(dve)
                nc.vector.bn_aggr(bn_m[:], bn_s[:].rearrange("d c s -> d (c s)")).then_inc(s_var, 1)
                dve.wait_ge(s_std, layer + 2)
                link(nc.vector.reciprocal(bn_r[:], bn_d[:]))
                link(nc.vector.tensor_tensor(bn_a[:], bn_r[:], gam[:, bass.ds(layer, 1)], ALU.mult))
                link(nc.vector.tensor_tensor(bn_t[:], bn_m[:, 0:1], bn_a[:], ALU.mult))
                link(nc.vector.tensor_tensor(bn_b[:], bet[:, bass.ds(layer, 1)], bn_t[:], ALU.subtract))
                assert taken[0] == BN_STEPS
                dve.sem_inc(s_bn, 1)
                set_weights(layer + 1)
                for c, u, n in node_chunks(dve, (layer + 1) * CHUNKS):
                    dve.wait_ge(s_root, n + (1 + CREDIT))
                    nc.vector.tensor_copy(rows[:, bass.ds(c * SUB, SUB), :], p_t[u % TURNS])
                    root_sum(layer + 1, c, u % TURNS)
                clear_tail()
                dve.wait_ge(s_node, (layer + 2) * CHUNKS + CREDIT)
                dve.sem_inc(s_rows, 1)
            segments(L - 1)
            dve.sem_inc(s_bn, 1)
            dve.wait_ge(s_x, 16)
            for c, u, n in node_chunks(dve, L * CHUNKS):
                dve.wait_ge(s_root, n + (1 + CREDIT))
                nc.vector.tensor_tensor(rows[:, bass.ds(c * SUB, SUB), :], p_t[u % TURNS],
                                        x_nm[:, bass.ds(c * SUB, SUB), :], ALU.add).then_inc(s_node, 1)
            dve.wait_ge(s_node, (L + 1) * CHUNKS + CREDIT)
            nc.vector.tensor_tensor(rows[:], rows[:], pb[:].unsqueeze(1).to_broadcast([NODE_P, PER, D]),
                                    ALU.add).then_inc(s_rows, 1)

        @block.scalar
        def _(act):
            act.wait_ge(s_var, 1)
            nc.scalar.activation(ln_v[:], ln_v[:], ACT.Sqrt, bias=eps[0:NODE_P, :], scale=1.0 / D).then_inc(s_std, 1)
            act.wait_ge(s_rows, 1)
            for c, u, n in node_chunks(act, 0):
                act.wait_ge(s_root, n + 1)
                nc.scalar.activation(stage[u][:], rows[:, bass.ds(c * SUB, SUB), :], ACT.Copy).then_inc(s_stage, 1)
                act.wait_ge(s_chT, n + 1)
                nc.scalar.activation(hT[u][:], p_h, ACT.Copy).then_inc(s_hT, 1)

            far = farthest(act)

            def copy_sums(s_sum, count, s_copied):
                act.wait_ge(s_sum, count)
                nc.scalar.activation(z[:], p_z, ACT.Copy).then_inc(s_copied, 1)

            def copy_transposed(s_trans, count, s_copied):
                act.wait_ge(s_trans, count)
                nc.scalar.activation(zT[:], p_zT, ACT.Copy)
                nc.scalar.activation(zxT[:], p_zxT, ACT.Copy).then_inc(s_copied, 1)

            def copy_segments_far(layer):
                with act.Fori(0, G) as g:
                    with act.Fori(0, FAR) as w:
                        m = (layer * G + g) * FAR + w
                        copy_sums(s_fseg, m + 1, s_fz)
                        copy_transposed(s_fT, m + 1, s_fzT)

            def compare_keys(layer, b, u, half):
                body = layer * BODIES + b + u // SLOTS
                k = layer * G + b * SLOTS + u
                u = u % SLOTS
                tiles = slice(half * HALF, (half + 1) * HALF)
                act.wait_ge(s_key[u], body * 16 + 16)
                act.wait_ge(s_pick, k * PICKED + (half + 1) * HALF)

                before = k * (4 * FOLD) + half * 2 * FOLD
                act.wait_ge(s_dist, before + 1)
                for f in range(FOLD):
                    nc.scalar.activation(distance[f][:], key[u % KEYS][:, tiles, :], ACT.Abs,
                                         bias=low_id[:, f:f + 1]).then_inc(s_dist, 1)
                for f in range(FOLD):
                    act.wait_ge(s_dist, before + f + 2)
                    nc.scalar.activation(low_hot[:, f, tiles, :], distance[f][:], ACT.Relu,
                                                bias=one[:], scale=-1.0).then_inc(s_dist, 1)
                act.wait_ge(s_dist, before + 2 * FOLD + 1)
                act.sem_inc(s_low, 1)

            def copy_rows(layer, b, u):
                k = layer * G + b * SLOTS + u
                act.wait_ge(s_gath[u], (layer * BODIES + b) * (16 * FETCHED) + 16 * FETCHED)
                act.wait_ge(s_xg, k * 2 + 3)
                act.wait_ge(s_seg, k + (CREDIT if u == 0 else CREDIT - 1))
                nc.scalar.activation(xp[u % PAIR][:, :, 0:D], xg[u][:], ACT.Copy).then_inc(s_xc, 1)

            def copy_segments(layer):
                for u, half in ((0, 0), (0, 1), (1, 0), (1, 1)):
                    compare_keys(layer, 0, u, half)
                for b, first, last in bodies(act):
                    for u in range(SLOTS):
                        k = layer * G + b * SLOTS + u
                        if not (first and u == 0):
                            copy_sums(s_seg, k + CREDIT, s_z)
                            copy_transposed(s_T, k, s_zT)
                        copy_rows(layer, b, u)
                        if not (last and u >= SLOTS - 2):
                            compare_keys(layer, b, u + 2, 0)
                            compare_keys(layer, b, u + 2, 1)
                copy_sums(s_seg, (layer + 1) * G + CREDIT, s_z)
                copy_transposed(s_T, (layer + 1) * G, s_zT)
                with act.If(far > WIN - 1):
                    copy_segments_far(layer)
                act.sem_inc(s_mark, 1)

            with act.Fori(0, L - 1) as layer:
                copy_segments(layer)
                act.wait_ge(s_var, layer + 2)
                nc.scalar.activation(bn_d[:], bn_m[:, 1:2], ACT.Sqrt, bias=eps[0:D, :]).then_inc(s_std, 1)
                act.wait_ge(s_bn, layer + 1)
                for c, u, n in node_chunks(act, (layer + 1) * CHUNKS):
                    act.wait_ge(s_root, n + 1)
                    nc.scalar.activation(hT[u][:], chunk_of(c), ACT.Relu, bias=bn_b[:], scale=bn_a[:]).then_inc(s_hT, 1)
            copy_segments(L - 1)
            act.wait_ge(s_bn, L)
            for c, u, n in node_chunks(act, L * CHUNKS):
                act.wait_ge(s_root, n + 1)
                nc.scalar.activation(hT[u][:], chunk_of(c), ACT.Relu).then_inc(s_hT, 1)

        @block.tensor
        def _(pe):
            for _ in range(PICKED):
                pe.sem_inc(s_pick, 1)
            for _ in range(CREDIT):
                pe.sem_inc(s_root, 1)
                pe.sem_inc(s_seg, 1)
            pe.wait_ge(s_ident, 1)
            pe.wait_ge(s_keyf, 1)
            flat = key_f.rearrange("p g j -> p (g j)")
            for c in range(PICKED):
                if c >= 2:
                    pe.wait_ge(s_key16, c - 1)
                nc.tensor.transpose(bank[c % 2][0:G, 0:P], flat[:, c * G:(c + 1) * G], ident[:]).then_inc(s_keyT, 1)
            pe.wait_ge(s_w, 1)
            for c, u, n in node_chunks(pe, 0):
                pe.wait_ge(s_stage, n + 1)
                for m in range(SUB):
                    last = nc.tensor.transpose(p_h[:, m, :], stage[u][:, m, :], ident[0:NODE_P, 0:NODE_P])
                last.then_inc(s_chT, 1)
                pe.wait_ge(s_hT, n + 1)
                pe.wait_ge(s_node, n + (CREDIT - 1))
                apart(pe)
                nc.tensor.matmul(p_r[u % TURNS], rw_now[:], hT[u][:], start=True, stop=True).then_inc(s_root, 1)

            far = farthest(pe)

            def sum_tiles(products, onehots):
                for j in range(TILES):
                    last = nc.tensor.matmul(p_z, onehots[:, j, :], products[:, j, :],
                                            start=j == 0, stop=j == TILES - 1)
                return last

            def transpose_sums():
                nc.tensor.transpose(p_zT, z[:, D:D + FD], ident[0:WIN, 0:WIN])
                return nc.tensor.transpose(p_zxT, z[:, 0:D], ident[0:WIN, 0:WIN])

            def messages():
                nc.tensor.matmul(p_agg, w_now[:], zT[:], start=True, stop=False)
                return nc.tensor.matmul(p_agg, eb_now[:], zxT[:], start=False, stop=True)

            def segment_sums_far(layer):
                with pe.Fori(0, G) as g:
                    pe.wait_ge(s_fprod, layer * G + g + 1)
                    apart(pe)
                    with pe.Fori(0, FAR) as w:
                        m = (layer * G + g) * FAR + w
                        pe.wait_ge(s_fhot, m + 1)
                        sum_tiles(xp[0], hot[0]).then_inc(s_fseg, 1)
                        pe.wait_ge(s_fz, m + 1)
                        transpose_sums().then_inc(s_fT, 1)
                        pe.wait_ge(s_fzT, m + 1)
                        messages().then_inc(s_fmm, 1)

            def pick(layer, b, u, t):
                k = layer * G + b * SLOTS + u
                if t % HALF == 0:
                    pe.wait_ge(s_low, k * 2 + (t // HALF + 1 + 2 * CREDIT))
                before = t - BANKS if t >= BANKS else max(range(t, PICKED, BANKS)) - PICKED
                pe.wait_ge(s_taken, k * PICKED + (before + 1 + PICKED))
                for f in range(FOLD):
                    for i in (1, 0):
                        last = nc.tensor.matmul(
                            p_sel[t % BANKS], low_hot[:, f, t, :],
                            nodes[i][:, f, :, :].rearrange("p f d -> p (f d)"),
                            start=(f, i) == (0, 1), stop=(f, i) == (FOLD - 1, 0))
                last.then_inc(s_pick, 1)

            def transposes_of(k):
                pe.wait_ge(s_z, k + 1)
                transpose_sums().then_inc(s_T, 1)

            def messages_of(k):
                pe.wait_ge(s_zT, k + 1)
                pe.wait_ge(s_add, k + CREDIT)
                messages().then_inc(s_mm, 1)

            def segment_sums(layer):
                pe.wait_ge(s_nodes, layer + 1)
                apart(pe)
                for t in range(PICKED):
                    pick(layer, 0, 0, t)
                for b, first, last in bodies(pe):
                    for u in range(SLOTS):
                        k = layer * G + b * SLOTS + u
                        for t in range(PICKED):
                            if not (last and u == SLOTS - 1):
                                pick(layer, b, u + 1, t)
                            if t == 1 and not (first and u == 0):
                                transposes_of(k - 1)
                            if t == 3 and not (first and u == 0):
                                messages_of(k - 1)
                        pe.wait_ge(s_hot, k + 1)
                        pe.wait_ge(s_xc, k + 1)
                        pe.wait_ge(s_prod, k + (1 + CREDIT))
                        sum_tiles(xp[u % PAIR], hot[u % PAIR]).then_inc(s_seg, 1)
                transposes_of(layer * G + (G - 1))
                messages_of(layer * G + (G - 1))
                with pe.If(far > WIN - 1):
                    segment_sums_far(layer)
                pe.sem_inc(s_mark, 1)

            with pe.Fori(0, L - 1) as layer:
                segment_sums(layer)
                pe.wait_ge(s_w, layer + 2)
                apart(pe)
                for c, u, n in node_chunks(pe, (layer + 1) * CHUNKS):
                    pe.wait_ge(s_hT, n + 1)
                    pe.wait_ge(s_node, n + (CREDIT - 1))
                    apart(pe)
                    for m in range(SUB):
                        nc.tensor.transpose(p_t[u % TURNS][:, m, :], hT[u][:, m, :], ident[0:D, 0:D])
                    nc.tensor.matmul(p_r[u % TURNS], rw_now[:], hT[u][:], start=True, stop=True).then_inc(s_root, 1)
            segment_sums(L - 1)
            for c, u, n in node_chunks(pe, L * CHUNKS):
                pe.wait_ge(s_hT, n + 1)
                pe.wait_ge(s_node, n + (CREDIT - 1))
                apart(pe)
                for m in range(SUB):
                    last = nc.tensor.matmul(p_t[u % TURNS][:, m, :], hT[u][:, m, :], pw[:], start=True, stop=True)
                last.then_inc(s_root, 1)


def kernel(**inputs):
    import numpy as _np
    import concourse.bacc as _bacc
    from concourse import mybir as _mybir
    from concourse.bass_utils import run_bass_kernel_spmd as _run

    w = {k.removeprefix("L0_gnn_"): _np.asarray(v) for k, v in inputs.items()}
    laid = {
        "x": w["x"], "src": w["src"], "dst": w["dst"], "edge_attr": w["edge_attr_8"],
        "edge_w": w["edge_w"], "edge_b": w["edge_b"], "root_w": w["root_w"],
        "root_b": w["root_b"].T, "gamma": w["bn_gamma"].T, "beta": w["bn_beta"].T,
        "pred_w": w["pred_w"], "pred_b": w["pred_b"],
    }
    nc = _bacc.Bacc("TRN2", target_bir_lowering=False, num_devices=1)
    arrays, args = {}, []
    for name, a in laid.items():
        a = _np.ascontiguousarray(a)
        arrays[f"in_{name}"] = a
        args.append(nc.dram_tensor(f"in_{name}", a.shape, _mybir.dt.from_np(a.dtype), kind="ExternalInput").ap())
    o = nc.dram_tensor("out_x", w["x"].shape, _mybir.dt.float32, kind="ExternalOutput").ap()
    gnn_kernel(nc, *args, o)
    r = _run(nc, [arrays], core_ids=[0])
    return r.results[0]["out_x"]
```

```python
from contextlib import ExitStack

import concourse.bass as bass
from concourse import mybir

P = 128
ALU = mybir.AluOpType
ACT = mybir.ActivationFunctionType
AX_X = mybir.AxisListType.X
F32 = mybir.dt.float32
F32R = mybir.dt.float32r
I16 = mybir.dt.int16
I32 = mybir.dt.int32

TILES = 25
PICKED = 8
FETCHED = TILES - PICKED
FOLD = 4
FOLD_BITS = 2
BANKS = 4
SLOTS = 5
PAIR = 2
CUT = 7
HALF = PICKED // 2
KEYS = 3
TURNS = 3
WIN = 112
NODE_P = 125
ROOM = 3
SUB = 4
EPS = 1e-5
CREDIT = SLOTS


def gnn_kernel(nc, x, src, dst, edge_attr, edge_w, edge_b, root_w, root_b, gamma, beta, pred_w, pred_b, out):
    N, D = x.shape
    E, F = edge_attr.shape
    L = edge_w.shape[0]
    FD = F * D
    GE = P * TILES
    G = E // GE
    BODIES = G // SLOTS
    PER = N // NODE_P
    CHUNKS = PER // SUB
    CN = NODE_P * SUB
    WINDOWS = -(-N // WIN)
    assert E == G * GE and G == BODIES * SLOTS and FD == P and D * (F + 1) <= 512
    assert N == NODE_P * PER and PER == CHUNKS * SUB and CHUNKS % SLOTS == 0 and CN <= 512

    FINE = -(-N // (P * FOLD))
    SELW = FINE * D
    assert SELW <= 512

    table = nc.dram_tensor("node_table", [N, D], F32, kind="Internal").ap()
    keys = nc.dram_tensor("edge_keys", [G * PICKED, P], I16, kind="Internal").ap()

    def parts(a, tail=""):
        v = a.rearrange(f"(g e) {tail} -> g e {tail}", g=G)
        return [w.rearrange(f"g (p j) {tail} -> g p j {tail}", p=P)
                for w in (v[:, 0:P * FETCHED], v[:, P * FETCHED:GE])]

    src_f, src_p = parts(src)
    dst_f, dst_p = parts(dst)
    ea_f, ea_p = parts(edge_attr, "f")
    cols_f, cols_p = slice(0, FETCHED), slice(FETCHED, TILES)

    with ExitStack() as ctx:
        def sb(name, shape, dt=F32):
            return ctx.enter_context(nc.sbuf_tensor(name, shape, dt))

        def ps(name, shape):
            return ctx.enter_context(nc.psum_tensor(name, shape, F32))

        def sem(name):
            return ctx.enter_context(nc.semaphore(name))

        idx = [sb(f"idx{u}", [P, FETCHED], I32) for u in range(SLOTS)]
        ea = [sb(f"ea{u}", [P, TILES, F]) for u in range(SLOTS)]
        xp = [sb(f"xp{i}", [P, TILES, D + FD]) for i in range(PAIR)]
        hot = [sb(f"hot{i}", [P, TILES, WIN], F32R) for i in range(PAIR)]
        cut_room = sb("cut_room", [P, ROOM, SUB * NODE_P])
        xcut = cut_room[:].rearrange("p a b -> p (a b)")[:, 0:CUT * (D + FD)].rearrange("p (a b) -> p a b", b=D + FD)
        xparts = sb("xparts", [P, CUT, 2, D + FD], F32R)
        xg = [sb(f"xg{u}", [P, TILES, D]) for u in range(SLOTS)]
        key = [sb(f"key{i}", [P, PICKED, P], I16) for i in range(KEYS)]
        low_hot = sb("low_hot", [P, FOLD, PICKED, P], F32R)
        low_id = sb("low_id", [P, FOLD])
        distance = [sb(f"distance{i}", [P, HALF, P], mybir.dt.bfloat16) for i in range(FOLD)]
        one = sb("one", [P, 1])
        fine = sb("fine", [P, G * PICKED])
        spread = sb("spread", [P, HALF, D, FINE])
        nodes = [sb(f"nodes{i}", [P, FOLD, FINE, D], F32R) for i in range(2)]
        nodes_raw, nodes_cut = (t[:].rearrange("p a b -> p (a b)")[:, 0:FOLD * SELW]
                                .rearrange("p (k f d) -> p k f d", k=FOLD, d=D) for t in xp)
        dst_rel = sb("dst_rel", [P, G, TILES])
        base_i = sb("base_i", [P, G], I32)
        far_i = sb("far_i", [P, 1], I32)
        scratch = xp[1][:].rearrange("p a b -> p (a b)")
        GP = G * PICKED
        assert PICKED == 2 * HALF and FOLD == 1 << FOLD_BITS and 3 * GP + PICKED * P // 2 <= TILES * (D + FD) and G <= P
        src_pick = scratch[:, 0:GP].bitcast(I32).rearrange("p (g j) -> p g j", g=G)
        src_int = scratch[:, GP:2 * GP].bitcast(I32).rearrange("p (g j) -> p g j", g=G)
        key_f = scratch[:, 2 * GP:3 * GP].rearrange("p (g j) -> p g j", g=G)
        key16 = scratch[0:G, 3 * GP:3 * GP + PICKED * P // 2].bitcast(I16).rearrange("q (c p) -> q c p", p=P)
        agg = sb("agg", [D, N + WIN])
        rows = sb("rows", [NODE_P, PER, D])
        x_nm = xp[0][0:NODE_P, :, :].rearrange("p a b -> p (a b)")[:, 0:PER * D].rearrange("p (m d) -> p m d", d=D)
        stage = [cut_room[0:NODE_P, 0, u * SUB * D:(u + 1) * SUB * D].rearrange("p (a b) -> p a b", b=D)
                 for u in range(SLOTS)]
        hT = [sb(f"hT{u}", [D, SUB, NODE_P]) for u in range(SLOTS - ROOM)]
        hT += [cut_room[0:D, i, :].rearrange("d (a b) -> d a b", b=NODE_P) for i in range(ROOM)]
        w_all = sb("w_all", [P, L, D])
        eb_all = sb("eb_all", [D, L, D])
        rw_all = sb("rw_all", [D, L, D])
        rb_all = sb("rb_all", [D, L])
        w_now = sb("w_now", [P, D])
        eb_now = sb("eb_now", [D, D])
        rw_now = sb("rw_now", [D, D])
        gam = sb("gam", [D, L - 1])
        bet = sb("bet", [D, L - 1])
        pw = sb("pw", [D, D])
        pb = sb("pb", [NODE_P, D])
        col_i = sb("col_i", [P, P], I32)
        row_i = sb("row_i", [P, 1], I32)
        low_id_i = sb("low_id_i", [P, FOLD], I32)
        col = sb("col", [P, P])
        row = sb("row", [P, 1])
        ident = sb("ident", [P, P])
        eps = sb("eps", [P, 1])
        z = sb("z", [WIN, D + FD])
        z_lower = sb("z_lower", [WIN, D + FD])
        zT = sb("zT", [P, WIN])
        zxT = sb("zxT", [D, WIN])
        low_p = col_i[:, 0:G].bitcast(F32)
        low_a = sb("low_a", [P, G])
        low_c = sb("low_c", [G, 1])
        low_d = sb("low_d", [G, G])
        ones = sb("ones", [P, P])
        far_p = sb("far_p", [P, 1])
        far_a = sb("far_a", [P, 1])
        ln_m = sb("ln_m", [NODE_P, PER])
        ln_v = sb("ln_v", [NODE_P, PER])
        ln_r = sb("ln_r", [NODE_P, PER])
        bn_s = sb("bn_s", [D, CHUNKS, 6])
        bn_m = sb("bn_m", [D, 2])
        bn_d = sb("bn_d", [D, 1])
        bn_r = sb("bn_r", [D, 1])
        bn_a = sb("bn_a", [D, 1])
        bn_t = sb("bn_t", [D, 1])
        bn_b = sb("bn_b", [D, 1])
        bn_diag = sb("bn_diag", [D, 2 * D])
        far_idx = sb("far_idx", [P, TILES], I32)
        far_ea = sb("far_ea", [P, TILES, F])
        far_rel = sb("far_rel", [P, TILES])
        far_col = sb("far_col", [P, 1])
        far_col_i = sb("far_col_i", [P, 1], I32)

        bank = [ps(f"bank{i}", [P, 512]) for i in range(8)]
        p_z, p_agg = bank[0][0:WIN, 0:D + FD], bank[2][0:D, 0:WIN]
        p_parts = bank[0][0:WIN, 0:2 * (D + FD)]
        p_zT, p_zxT = bank[1][:, 0:WIN], bank[1][0:D, WIN:2 * WIN]
        p_sel = [bank[3 + i][:, 0:SELW] for i in range(BANKS)]
        p_t = [bank[i][0:NODE_P, 0:SUB * D].rearrange("p (m d) -> p m d", d=D) for i in range(TURNS)]
        p_norm = bank[6][0:NODE_P, 0:2 * D]
        p_r = [bank[i][0:D, 0:CN].rearrange("d (m p) -> d m p", m=SUB) for i in range(TURNS, 2 * TURNS)]

        s_const = sem("const_loaded")
        s_dst = sem("dst_loaded")
        s_iota = sem("iota_done")
        s_v = sem("vector_step")
        s_base = sem("base_step")
        s_baseT = sem("base_step_of_tensor")
        s_flag = sem("flag_ready")
        s_ident = sem("ident_ready")
        s_var = sem("variance_ready")
        s_std = sem("std_ready")
        s_rows = sem("rows_ready")
        s_table = sem("table_written")
        s_w = sem("weights_set")
        s_stats = sem("chunk_stats")
        s_bn = sem("norm_ready")
        s_first = sem("chunk_in_agg")
        s_stage = sem("chunk_staged")
        s_chT = sem("chunk_transposed")
        s_hT = sem("chunk_normed")
        s_root = sem("chunk_products")
        s_sum = sem("layer_summed")
        s_diag = sem("norm_on_diagonals")
        s_norm = sem("norm_spread")
        s_node = sem("chunk_done")
        s_idx = [sem(f"edges_loaded{u}") for u in range(SLOTS)]
        s_gath = [sem(f"gathered{u}") for u in range(SLOTS)]
        s_src = sem("picked_sources_loaded")
        s_keyf = sem("keys_in_float")
        s_keyT = sem("keys_transposed")
        s_key16 = sem("keys_in_int16")
        s_keyd = sem("keys_written")
        s_key = [sem(f"keys_loaded{u}") for u in range(SLOTS)]
        s_nload = sem("nodes_loaded")
        s_tail = sem("tail_cleared")
        s_split = sem("upper_parts_ready")
        s_nodes = sem("nodes_split")
        s_dist = sem("distances_ready")
        s_low = sem("low_onehot_ready")
        s_pick = sem("tile_picked")
        s_taken = sem("pick_taken")
        s_xg = sem("picks_summed")
        s_xc = sem("rows_copied")
        s_hot = sem("onehot_ready")
        s_prod = sem("products_ready")
        s_seg = sem("segments_summed")
        s_cut = sem("products_cut")
        s_upper = sem("upper_parts_set")
        s_lower = sem("lower_parts_set")
        s_zl = sem("lower_sums_copied")
        s_z = sem("sums_joined")
        s_T = sem("sums_transposed")
        s_zT = sem("transposed_copied")
        s_mm = sem("messages_ready")
        s_add = sem("messages_added")
        s_x = sem("x_loaded")
        s_out = sem("output_written")
        s_mark = sem("wait_passed")
        s_fgo = sem("far_group_begun")
        s_fload = sem("far_edges_loaded")
        s_fgath = sem("far_gathered")
        s_fprod = sem("far_products_ready")
        s_fv = sem("far_vector_step")
        s_fhot = sem("far_onehot_ready")
        s_fseg = sem("far_segments_summed")
        s_fz = sem("far_sums_copied")
        s_fT = sem("far_sums_transposed")
        s_fzT = sem("far_transposed_copied")
        s_fmm = sem("far_messages_ready")
        s_fadd = sem("far_messages_added")

        block = ctx.enter_context(nc.Block())

        def chunk_of(c):
            return agg[:, 0:N].rearrange("d (p m) -> d m p", m=PER)[:, bass.ds(c * SUB, SUB), :]

        def bodies(eng):
            yield 0, True, False
            with eng.Fori(1, BODIES - 1) as b:
                yield b, False, False
            yield BODIES - 1, False, True

        def node_chunks(eng, n0):
            with eng.Fori(0, CHUNKS // SLOTS) as cb:
                for u in range(SLOTS):
                    yield cb * SLOTS + u, u, n0 + cb * SLOTS + u

        def apart(eng):
            eng.sem_inc(s_mark, 1)

        FAR = WINDOWS - 1

        def farthest(eng):
            eng.wait_ge(s_flag, 1)
            return eng.value_load(far_i[0:1, 0:1], min_val=0, max_val=N)

        @block.sync
        def _(sp):
            sp.dma_start(x_nm, x.rearrange("(p m) d -> p m d", m=PER)).then_inc(s_x, 16)
            sp.dma_start(w_all[:], edge_w.rearrange("l f (i o) -> (f i) l o", o=D)).then_inc(s_const, 16)
            sp.dma_start(eb_all[:], edge_b.rearrange("l (i o) -> i l o", o=D)).then_inc(s_const, 16)
            sp.dma_start(rw_all[:], root_w.rearrange("l i o -> i l o")).then_inc(s_const, 16)
            sp.dma_start(rb_all[:], root_b).then_inc(s_const, 16)
            sp.dma_start(gam[:], gamma).then_inc(s_const, 16)
            sp.dma_start(bet[:], beta).then_inc(s_const, 16)
            sp.dma_start(pw[:], pred_w).then_inc(s_const, 16)
            sp.dma_start(pb[:], pred_b[None, :].to_broadcast([NODE_P, D])).then_inc(s_const, 16)

            def write_table(layer):
                sp.wait_ge(s_rows, layer + 1)
                sp.dma_start(table.rearrange("(p m) d -> p m d", m=PER), rows[:]).then_inc(s_table, 16)
                sp.wait_ge(s_table, layer * 16 + 16)
                sp.wait_ge(s_tail, layer + 1)
                whole = N // P
                by_block = table[0:whole * P, :].rearrange("(m p) d -> p m d", p=P)
                for k in range(FOLD):
                    count = len(range(k, whole, FOLD))
                    sp.dma_start(nodes_raw[:, k, 0:count, :], by_block[:, k::FOLD, :]).then_inc(s_nload, 16)
                sp.dma_start(nodes_raw[0:N - whole * P, whole % FOLD, whole // FOLD, :],
                             table[whole * P:N, :]).then_inc(s_nload, 16)

            def load_far(layer):
                with sp.Fori(0, G) as g:
                    n = layer * G + g
                    sp.wait_ge(s_fgo, n + 1)
                    for cols, of_src, of_ea in ((cols_f, src_f, ea_f), (cols_p, src_p, ea_p)):
                        sp.dma_start(far_idx[:, cols], of_src[bass.ds(g, 1), :, :]
                                     .rearrange("g p j -> (g p) j")).then_inc(s_fload, 16)
                        sp.dma_start(far_ea[:, cols, :], of_ea[bass.ds(g, 1), :, :, :]
                                     .rearrange("g p j f -> (g p) j f")).then_inc(s_fload, 16)

            def load_edges(layer, b, u):
                sp.wait_ge(s_prod, layer * G + b * SLOTS + (u + 1))
                g = bass.ds(b * SLOTS + u, 1)
                sp.dma_start(idx[u][:], src_f[g, :, :].rearrange("g p j -> (g p) j")).then_inc(s_idx[u], 16)
                sp.dma_start(ea[u][:, cols_f, :], ea_f[g, :, :, :]
                             .rearrange("g p j f -> (g p) j f")).then_inc(s_idx[u], 16)
                sp.dma_start(ea[u][:, cols_p, :], ea_p[g, :, :, :]
                             .rearrange("g p j f -> (g p) j f")).then_inc(s_idx[u], 16)

            def load_keys(layer, b, u):
                sp.wait_ge(s_keyd, 16)
                sp.wait_ge(s_low, (layer * G + b * SLOTS) * 2 + (2 * u + 2 * CREDIT - 2))
                sp.dma_start(
                    key[u % KEYS][:].rearrange("p t e -> p (t e)"),
                    keys[bass.ds((b * SLOTS + u) * PICKED, PICKED), :].rearrange("(a t) e -> a (t e)", a=1)
                    .to_broadcast([P, PICKED * P])).then_inc(s_key[u], 16)

            AHEAD = 2

            def load_others(layer):
                for u in range(AHEAD, SLOTS):
                    load_keys(layer, 0, u)
                with sp.Fori(1, BODIES) as b:
                    for u in range(SLOTS):
                        load_edges(layer, b, u)
                        load_keys(layer, b, u)
                far = farthest(sp)
                with sp.If(far > WIN - 1):
                    load_far(layer)
                sp.sem_inc(s_mark, 1)

            for u in range(SLOTS):
                load_edges(0, 0, u)
            write_table(0)
            for u in range(AHEAD):
                load_keys(0, 0, u)
            with sp.Fori(0, L - 1) as layer:
                load_others(layer)
                for u in range(SLOTS):
                    load_edges(layer + 1, 0, u)
                for u in range(AHEAD):
                    load_keys(layer + 1, 0, u)
                write_table(layer + 1)
            load_others(L - 1)
            sp.wait_ge(s_bn, L)
            sp.dma_start(x_nm, x.rearrange("(p m) d -> p m d", m=PER)).then_inc(s_x, 16)
            sp.wait_ge(s_rows, L + 1)
            sp.dma_start(out.rearrange("(p m) d -> p m d", m=PER), rows[:]).then_inc(s_out, 16)
            sp.wait_ge(s_out, 16)

        @block.gpsimd
        def _(pool):
            pool.iota(col_i[:], [[1, P]], base=0, channel_multiplier=0).then_inc(s_iota, 1)
            pool.iota(row_i[:], [[0, 1]], base=0, channel_multiplier=1).then_inc(s_iota, 1)
            for k in range(FOLD):
                pool.iota(low_id_i[:, k:k + 1], [[0, 1]], base=k * P, channel_multiplier=1).then_inc(s_iota, 1)
            def gather_far(layer):
                with pool.Fori(0, G) as g:
                    pool.wait_ge(s_fload, (layer * G + g) * 64 + 64)
                    apart(pool)
                    for j in range(TILES):
                        pool.indirect_dma_start(
                            out=xp[0][:, j, 0:D], out_offset=None, in_=table[:, :],
                            in_offset=bass.IndirectOffsetOnAxis(ap=far_idx[:, j:j + 1], axis=0),
                        ).then_inc(s_fgath, 16)

            def gather(layer):
                pool.wait_ge(s_table, layer * 16 + 16)
                apart(pool)
                with pool.Fori(0, BODIES) as b:
                    for u in range(SLOTS):
                        pool.wait_ge(s_idx[u], (layer * BODIES + b) * 48 + 48)
                        pool.wait_ge(s_seg, layer * G + b * SLOTS + (u + 1))
                        apart(pool)
                        for j in range(FETCHED):
                            pool.indirect_dma_start(
                                out=xg[u][:, j, :], out_offset=None, in_=table[:, :],
                                in_offset=bass.IndirectOffsetOnAxis(ap=idx[u][:, j:j + 1], axis=0),
                            ).then_inc(s_gath[u], 16)
                far = farthest(pool)
                with pool.If(far > WIN - 1):
                    gather_far(layer)
                pool.sem_inc(s_mark, 1)

            with pool.Fori(0, L - 1) as layer:
                gather(layer)
            gather(L - 1)

        @block.vector
        def _(dve):
            steps = [0]

            def step(ins):
                steps[0] += 1
                ins.then_inc(s_v, 1)
                dve.wait_ge(s_v, steps[0])

            dve.sem_inc(s_xg, 1)
            dve.sem_inc(s_dist, 1)
            for _ in range(2 * CREDIT):
                dve.sem_inc(s_low, 1)
            for _ in range(PICKED):
                dve.sem_inc(s_taken, 1)
            def clear_tail():
                nc.vector.memset(nodes_raw[:, :, N // (P * FOLD):FINE, :], 0.0).then_inc(s_tail, 1)

            for _ in range(CREDIT):
                dve.sem_inc(s_prod, 1)
                dve.sem_inc(s_add, 1)
                dve.sem_inc(s_node, 1)
            dve.wait_ge(s_iota, 2 + FOLD)
            nc.vector.tensor_scalar(low_id[:], low_id_i[:], -1.0, None, ALU.mult)
            nc.vector.memset(one[:], 1.0)
            nc.vector.tensor_copy(col[:], col_i[:])
            nc.vector.memset(eps[:], EPS)
            nc.vector.memset(agg[:, N:N + WIN], 0.0)
            step(nc.vector.tensor_copy(row[:], row_i[:]))
            nc.vector.tensor_scalar(ident[:], col[:], row[:, 0:1], None, ALU.is_equal).then_inc(s_ident, 1)

            dve.wait_ge(s_x, 16)
            step(nc.vector.tensor_reduce(ln_m[:], x_nm, AX_X, ALU.add))
            step(nc.vector.tensor_scalar(ln_m[:], ln_m[:], 1.0 / D, None, ALU.mult))
            ln_mb = ln_m[:].unsqueeze(2).to_broadcast([NODE_P, PER, D])
            step(nc.vector.tensor_tensor(rows[:], x_nm, ln_mb, ALU.subtract))
            squares = (spread[0:NODE_P, :, :, :].rearrange("p a b c -> p (a b c)")[:, 0:PER * D]
                       .rearrange("p (m d) -> p m d", d=D))
            step(nc.vector.tensor_tensor(squares, rows[:], rows[:], ALU.mult))
            nc.vector.tensor_reduce(ln_v[:], squares, AX_X, ALU.add).then_inc(s_var, 1)
            dve.wait_ge(s_std, 1)
            step(nc.vector.reciprocal(ln_r[:], ln_v[:]))
            ln_rb = ln_r[:].unsqueeze(2).to_broadcast([NODE_P, PER, D])
            step(nc.vector.tensor_tensor(rows[:], rows[:], ln_rb, ALU.mult))
            clear_tail()
            nc.vector.tensor_scalar(rows[:], rows[:], 0.0, None, ALU.max).then_inc(s_rows, 1)

            dve.wait_ge(s_src, 16)
            step(nc.vector.tensor_scalar(src_int, src_pick, 7 + FOLD_BITS, None, ALU.logical_shift_right))
            step(nc.vector.tensor_copy(fine[:].rearrange("p (g j) -> p g j", g=G), src_int))
            step(nc.vector.tensor_scalar(src_int, src_pick, P * FOLD - 1, None, ALU.bitwise_and))
            nc.vector.tensor_copy(key_f, src_int).then_inc(s_keyf, 1)
            for c in range(PICKED):
                dve.wait_ge(s_keyT, c + 1)
                nc.vector.tensor_copy(key16[:, c, :], bank[c % 2][0:G, 0:P]).then_inc(s_key16, 1)

            dve.wait_ge(s_dst, 32)
            step(nc.vector.tensor_copy(dst_rel[:], dst_rel[:].bitcast(I32)))
            step(nc.vector.tensor_reduce(low_p[:], dst_rel[:], AX_X, ALU.min))
            step(nc.vector.memset(ones[:], 1.0))
            dve.sem_inc(s_base, 1)
            dve.wait_ge(s_baseT, 1)
            step(nc.vector.tensor_reduce(low_c[:], bank[0][0:G, 0:P], AX_X, ALU.min))
            nc.vector.tensor_scalar(low_d[:], ident[0:G, 0:G], low_c[:], None, ALU.mult).then_inc(s_base, 1)
            dve.wait_ge(s_baseT, 2)
            nc.vector.tensor_copy(base_i[:], bank[1][:, 0:G])
            step(nc.vector.tensor_copy(low_a[:], bank[1][:, 0:G]))
            low_b = low_a[:].unsqueeze(2).to_broadcast([P, G, TILES])
            step(nc.vector.tensor_tensor(dst_rel[:], dst_rel[:], low_b, ALU.subtract))
            nc.vector.tensor_reduce(far_p[:], dst_rel[:].rearrange("p g j -> p (g j)"), AX_X,
                                    ALU.max).then_inc(s_base, 1)
            dve.wait_ge(s_baseT, 3)
            step(nc.vector.tensor_reduce(far_a[0:1, :], bank[0][0:1, 0:P], AX_X, ALU.max))
            nc.vector.tensor_copy(far_i[0:1, :], far_a[0:1, :]).then_inc(s_flag, 1)

            def set_weights(layer):
                nc.vector.tensor_copy(w_now[:], w_all[:, bass.ds(layer, 1), :].rearrange("p l o -> p (l o)"))
                nc.vector.tensor_copy(eb_now[:], eb_all[:, bass.ds(layer, 1), :].rearrange("p l o -> p (l o)"))
                nc.vector.tensor_copy(rw_now[:], rw_all[:, bass.ds(layer, 1), :].rearrange("p l o -> p (l o)")
                                      ).then_inc(s_w, 1)

            def root_sums(layer):
                for c, u, n in node_chunks(dve, layer * 2 * CHUNKS):
                    dve.wait_ge(s_root, n + (1 + CREDIT))
                    nc.vector.tensor_scalar(chunk_of(c), p_r[u % TURNS], rb_all[:, bass.ds(layer, 1)], None,
                                            ALU.add).then_inc(s_node, 1)
                dve.wait_ge(s_node, (layer * 2 + 1) * CHUNKS + CREDIT)
                apart(dve)

            def segments_far(layer):
                with dve.Fori(0, G) as g:
                    n = layer * G + g
                    done = n * (1 + 3 * FAR)
                    dve.sem_inc(s_fgo, 1)
                    nc.vector.tensor_copy(far_rel[:], dst_rel[:, bass.ds(g, 1), :].rearrange("p g j -> p (g j)"))
                    nc.vector.tensor_copy(far_col[:], low_a[:, bass.ds(g, 1)]).then_inc(s_fv, 1)
                    dve.wait_ge(s_fload, n * 64 + 64)
                    dve.wait_ge(s_fgath, n * (16 * TILES) + 16 * TILES)
                    products(xp[0], xp[0][:, :, 0:D], far_ea).then_inc(s_fprod, 1)
                    with dve.Fori(0, FAR) as w:
                        m = n * FAR + w
                        dve.wait_ge(s_fv, done + w * 3 + 1)
                        nc.vector.tensor_scalar(far_rel[:], far_rel[:], -float(WIN), None, ALU.add).then_inc(s_fv, 1)
                        nc.vector.tensor_scalar(far_col[:], far_col[:], float(WIN), float(N), ALU.add,
                                                ALU.min).then_inc(s_fv, 1)
                        dve.wait_ge(s_fv, done + w * 3 + 3)
                        onehots(hot[0], far_rel[:]).then_inc(s_fhot, 1)
                        nc.vector.tensor_copy(far_col_i[:], far_col[:]).then_inc(s_fv, 1)
                        dve.wait_ge(s_fv, done + w * 3 + 4)
                        apart(dve)
                        base = dve.value_load(far_col_i[0:1, 0:1], min_val=0, max_val=N)
                        here = agg[:, bass.ds(base, WIN)]
                        dve.wait_ge(s_fmm, m + 1)
                        nc.vector.tensor_tensor(here, here, p_agg, ALU.add).then_inc(s_fadd, 1)
                        dve.wait_ge(s_fadd, m + 1)
                        apart(dve)

            def onehots(buf, rel):
                return nc.vector.tensor_tensor(
                    buf[:], col[:, 0:WIN].unsqueeze(1).to_broadcast([P, TILES, WIN]),
                    rel.unsqueeze(2).to_broadcast([P, TILES, WIN]), ALU.is_equal)

            def products(buf, rows_of, features):
                xj = rows_of.unsqueeze(2).to_broadcast([P, TILES, F, D])
                ef = features[:].unsqueeze(3).to_broadcast([P, TILES, F, D])
                return nc.vector.tensor_tensor(
                    buf[:, :, D:D + FD].rearrange("p j (f d) -> p j f d", d=D), xj, ef, ALU.mult)

            def split_nodes(layer):
                dve.wait_ge(s_keyd, 16)
                dve.wait_ge(s_nload, (layer + 1) * (16 * (FOLD + 1)))
                nc.vector.tensor_scalar(nodes_cut.bitcast(I32), nodes_raw.bitcast(I32), -(1 << 12), None,
                                        ALU.bitwise_and).then_inc(s_split, 1)
                dve.wait_ge(s_split, layer + 1)
                nc.vector.tensor_copy(nodes[1][:], nodes_cut)
                nc.vector.tensor_tensor(nodes[0][:], nodes_raw, nodes_cut, ALU.subtract).then_inc(s_nodes, 1)
                dve.wait_ge(s_nodes, layer + 1)

            def compare_targets(layer, b, u):
                k = layer * G + b * SLOTS + u
                dve.wait_ge(s_seg, k + (CREDIT if u % SLOTS == 0 else CREDIT - 1))
                rel = dst_rel[:, bass.ds(b * SLOTS + u, 1), :].rearrange("p g j -> p (g j)")
                onehots(hot[u % SLOTS % PAIR], rel).then_inc(s_hot, 1)

            def take_picks(layer, b, u, half):
                k = layer * G + b * SLOTS + u
                t0, t1 = half * HALF, (half + 1) * HALF
                for t in range(t0, t1):
                    n = k * PICKED + t
                    dve.wait_ge(s_pick, n + (1 + PICKED))
                    if t == t0:
                        dve.wait_ge(s_xg, k * 2 + (half + 1))
                    nc.vector.scalar_tensor_tensor(
                        spread[:, t - t0, :, :].rearrange("p d f -> p f d"),
                        col[:, 0:FINE].unsqueeze(2).to_broadcast([P, FINE, D]),
                        fine[:, bass.ds((b * SLOTS + u) * PICKED + t, 1)],
                        p_sel[t % BANKS].rearrange("p (f d) -> p f d", d=D),
                        ALU.is_equal, ALU.mult).then_inc(s_taken, 1)
                dve.wait_ge(s_taken, k * PICKED + (t1 + PICKED))
                nc.vector.tensor_reduce(xg[u % SLOTS][:, FETCHED + t0:FETCHED + t1, :], spread[:, 0:t1 - t0, :, :],
                                        AX_X, ALU.add).then_inc(s_xg, 1)

            def multiply(layer, b, u):
                k = layer * G + b * SLOTS + u
                body = layer * BODIES + b
                dve.wait_ge(s_idx[u], body * 48 + 48)
                dve.wait_ge(s_gath[u], body * (16 * FETCHED) + 16 * FETCHED)
                dve.wait_ge(s_xg, k * 2 + 3)
                dve.wait_ge(s_seg, k + (CREDIT if u == 0 else CREDIT - 1))
                products(xp[u % PAIR], xg[u][:], ea[u]).then_inc(s_prod, 1)

            def cut_upper(layer, b, u):
                k = layer * G + b * SLOTS + u
                dve.wait_ge(s_xc, k + 1)
                dve.wait_ge(s_prod, k + (1 + CREDIT))
                nc.vector.tensor_scalar(xcut.bitcast(I32), xp[u % PAIR][:, 0:CUT, :].bitcast(I32), -(1 << 12), None,
                                        ALU.bitwise_and).then_inc(s_cut, 1)

            def take_lower(layer, b, u):
                k = layer * G + b * SLOTS + u
                dve.wait_ge(s_cut, k + 1)
                dve.wait_ge(s_seg, k + CREDIT)
                nc.vector.tensor_tensor(xparts[:, :, 1, :], xp[u % PAIR][:, 0:CUT, :], xcut,
                                        ALU.subtract).then_inc(s_lower, 1)

            def join(k):
                dve.wait_ge(s_zl, k + 1)
                nc.vector.tensor_tensor(z[:], z_lower[:], p_z, ALU.add).then_inc(s_z, 1)

            def add(layer, b, u):
                k = layer * G + b * SLOTS + u
                base = dve.value_load(base_i[0:1, bass.ds(b * SLOTS + u, 1)], min_val=0, max_val=N - 1)
                here = agg[:, bass.ds(base, WIN)]
                dve.wait_ge(s_mm, k + 1)
                dve.wait_ge(s_add, k + CREDIT)
                nc.vector.tensor_tensor(here, here, p_agg, ALU.add).then_inc(s_add, 1)

            def segments(layer):
                take_picks(layer, 0, 0, 0)
                take_picks(layer, 0, 0, 1)
                for b, first, last in bodies(dve):
                    for u in range(SLOTS):
                        another = not (last and u == SLOTS - 1)
                        early = (u + 1) % SLOTS != 0
                        multiply(layer, b, u)
                        if not (first and u == 0):
                            join(layer * G + b * SLOTS + u - 1)
                        if another:
                            take_picks(layer, b, u + 1, 0)
                        cut_upper(layer, b, u)
                        take_lower(layer, b, u)
                        if another:
                            if early:
                                compare_targets(layer, b, u + 1)
                            take_picks(layer, b, u + 1, 1)
                        if not (first and u == 0):
                            add(layer, b, u - 1)
                        if another and not early:
                            compare_targets(layer, b, u + 1)
                join(layer * G + (G - 1))
                add(layer, BODIES - 1, SLOTS - 1)
                dve.wait_ge(s_add, layer * G + (G + CREDIT))
                apart(dve)
                far = farthest(dve)
                with dve.If(far > WIN - 1):
                    segments_far(layer)
                dve.sem_inc(s_mark, 1)

            dve.wait_ge(s_const, 8 * 16)
            set_weights(0)
            compare_targets(0, 0, 0)
            split_nodes(0)
            root_sums(0)

            BN_STEPS = 6
            with dve.Fori(0, L - 1) as layer:
                segments(layer)
                taken = [0]

                def link(ins):
                    taken[0] += 1
                    ins.then_inc(s_v, 1)
                    dve.wait_ge(s_v, layer * BN_STEPS + (steps[0] + taken[0]))

                dve.sem_inc(s_sum, 1)
                clear_tail()
                for c, u, n in node_chunks(dve, (layer * 2 + 1) * CHUNKS):
                    nc.vector.bn_stats(bn_s[:, bass.ds(c, 1), :].rearrange("d c s -> d (c s)"),
                                       agg[:, bass.ds(c * CN, CN)]).then_inc(s_stats, 1)
                    dve.wait_ge(s_root, n + (1 + CREDIT))
                    nc.vector.tensor_copy(rows[:, bass.ds(c * SUB, SUB), :], p_t[u % TURNS]).then_inc(s_node, 1)
                dve.wait_ge(s_stats, layer * CHUNKS + CHUNKS)
                apart(dve)
                nc.vector.bn_aggr(bn_m[:], bn_s[:].rearrange("d c s -> d (c s)")).then_inc(s_var, 1)
                dve.wait_ge(s_std, layer + 2)
                link(nc.vector.reciprocal(bn_r[:], bn_d[:]))
                link(nc.vector.tensor_tensor(bn_a[:], bn_r[:], gam[:, bass.ds(layer, 1)], ALU.mult))
                link(nc.vector.tensor_tensor(bn_t[:], bn_m[:, 0:1], bn_a[:], ALU.mult))
                link(nc.vector.tensor_tensor(bn_b[:], bet[:, bass.ds(layer, 1)], bn_t[:], ALU.subtract))
                dve.sem_inc(s_bn, 1)
                nc.vector.tensor_scalar(bn_diag[:, 0:D], ident[0:D, 0:D], bn_a[:], None, ALU.mult)
                nc.vector.tensor_scalar(bn_diag[:, D:2 * D], ident[0:D, 0:D], bn_b[:], None,
                                        ALU.mult).then_inc(s_diag, 1)
                set_weights(layer + 1)
                dve.wait_ge(s_norm, layer + 1)
                dve.wait_ge(s_node, (layer * 2 + 2) * CHUNKS + CREDIT)
                apart(dve)
                scale, shift = (p_norm[:, i * D:(i + 1) * D].unsqueeze(1).to_broadcast([NODE_P, PER, D])
                                for i in range(2))
                link(nc.vector.tensor_tensor(rows[:], rows[:], scale, ALU.mult))
                link(nc.vector.tensor_tensor(rows[:], rows[:], shift, ALU.add))
                assert taken[0] == BN_STEPS
                nc.vector.tensor_scalar(rows[:], rows[:], 0.0, None, ALU.max).then_inc(s_rows, 1)
                compare_targets(layer + 1, 0, 0)
                root_sums(layer + 1)
                split_nodes(layer + 1)
            segments(L - 1)
            dve.sem_inc(s_bn, 1)
            dve.wait_ge(s_x, 32)
            for c, u, n in node_chunks(dve, (2 * L - 1) * CHUNKS):
                dve.wait_ge(s_root, n + (1 + CREDIT))
                nc.vector.tensor_tensor(rows[:, bass.ds(c * SUB, SUB), :], p_t[u % TURNS],
                                        x_nm[:, bass.ds(c * SUB, SUB), :], ALU.add).then_inc(s_node, 1)
            dve.wait_ge(s_node, 2 * L * CHUNKS + CREDIT)
            nc.vector.tensor_tensor(rows[:], rows[:], pb[:].unsqueeze(1).to_broadcast([NODE_P, PER, D]),
                                    ALU.add).then_inc(s_rows, 1)

        @block.scalar
        def _(act):
            act.dma_start(src_pick, src_p.rearrange("g p j -> p g j")).then_inc(s_src, 16)
            dst_i = dst_rel[:].bitcast(I32)
            act.dma_start(dst_i[:, :, cols_f], dst_f.rearrange("g p j -> p g j")).then_inc(s_dst, 16)
            act.dma_start(dst_i[:, :, cols_p], dst_p.rearrange("g p j -> p g j")).then_inc(s_dst, 16)
            act.wait_ge(s_var, 1)
            nc.scalar.activation(ln_v[:], ln_v[:], ACT.Sqrt, bias=eps[0:NODE_P, :], scale=1.0 / D).then_inc(s_std, 1)
            act.wait_ge(s_rows, 1)
            with act.Fori(0, CHUNKS // SLOTS) as cb:
                for u in range(SLOTS):
                    c = cb * SLOTS + u
                    nc.scalar.activation(stage[u], rows[:, bass.ds(c * SUB, SUB), :], ACT.Copy).then_inc(s_stage, 1)
                for u in range(SLOTS):
                    c = cb * SLOTS + u
                    act.wait_ge(s_chT, cb * SLOTS + (u + 1))
                    nc.scalar.activation(chunk_of(c), p_r[u % TURNS], ACT.Copy).then_inc(s_first, 1)
            act.wait_ge(s_key16, PICKED)
            act.dma_start(keys.rearrange("(c q) p -> q c p", q=G), key16).then_inc(s_keyd, 16)
            act.wait_ge(s_first, CHUNKS)

            def normed(number, function=ACT.Relu, **norm):
                for c, u, n in node_chunks(act, number * CHUNKS):
                    act.wait_ge(s_root, n + 1)
                    nc.scalar.activation(hT[u][:], chunk_of(c), function, **norm).then_inc(s_hT, 1)

            normed(0)

            def copy_lower(k):
                act.wait_ge(s_seg, k + (1 + CREDIT))
                nc.scalar.activation(z_lower[:], p_parts[:, D + FD:], ACT.Copy).then_inc(s_zl, 1)

            def copy_upper(k):
                act.wait_ge(s_cut, k + 1)
                nc.scalar.activation(xparts[:, :, 0, :], xcut, ACT.Copy).then_inc(s_upper, 1)

            def copy_transposed(s_trans, count, s_copied):
                act.wait_ge(s_trans, count)
                nc.scalar.activation(zT[:], p_zT, ACT.Copy)
                nc.scalar.activation(zxT[:], p_zxT, ACT.Copy).then_inc(s_copied, 1)

            def copy_segments_far(layer):
                with act.Fori(0, G) as g:
                    with act.Fori(0, FAR) as w:
                        m = (layer * G + g) * FAR + w
                        act.wait_ge(s_fseg, m + 1)
                        nc.scalar.activation(z[:], p_z, ACT.Copy).then_inc(s_fz, 1)
                        copy_transposed(s_fT, m + 1, s_fzT)

            def compare_keys(layer, b, u, half):
                body = layer * BODIES + b + u // SLOTS
                k = layer * G + b * SLOTS + u
                u = u % SLOTS
                tiles = slice(half * HALF, (half + 1) * HALF)
                act.wait_ge(s_key[u], body * 16 + 16)
                act.wait_ge(s_pick, k * PICKED + (half + 1) * HALF)

                before = k * (4 * FOLD) + half * 2 * FOLD
                act.wait_ge(s_dist, before + 1)
                for f in range(FOLD):
                    nc.scalar.activation(distance[f][:], key[u % KEYS][:, tiles, :], ACT.Abs,
                                         bias=low_id[:, f:f + 1]).then_inc(s_dist, 1)
                for f in range(FOLD):
                    act.wait_ge(s_dist, before + f + 2)
                    nc.scalar.activation(low_hot[:, f, tiles, :], distance[f][:], ACT.Relu,
                                                bias=one[:], scale=-1.0).then_inc(s_dist, 1)
                act.wait_ge(s_dist, before + 2 * FOLD + 1)
                act.sem_inc(s_low, 1)

            def copy_rows(layer, b, u):
                k = layer * G + b * SLOTS + u
                act.wait_ge(s_gath[u], (layer * BODIES + b) * (16 * FETCHED) + 16 * FETCHED)
                act.wait_ge(s_xg, k * 2 + 3)
                act.wait_ge(s_seg, k + (CREDIT if u == 0 else CREDIT - 1))
                nc.scalar.activation(xp[u % PAIR][:, :, 0:D], xg[u][:], ACT.Copy).then_inc(s_xc, 1)

            def copy_segments(layer):
                for u, half in ((0, 0), (0, 1), (1, 0), (1, 1)):
                    compare_keys(layer, 0, u, half)
                for b, first, last in bodies(act):
                    for u in range(SLOTS):
                        k = layer * G + b * SLOTS + u
                        if not (first and u == 0):
                            copy_lower(k - 1)
                        copy_rows(layer, b, u)
                        if not (first and u == 0):
                            copy_transposed(s_T, k, s_zT)
                        copy_upper(k)
                        if not (last and u >= SLOTS - 2):
                            compare_keys(layer, b, u + 2, 0)
                            compare_keys(layer, b, u + 2, 1)
                copy_lower(layer * G + (G - 1))
                copy_transposed(s_T, (layer + 1) * G, s_zT)
                far = farthest(act)
                with act.If(far > WIN - 1):
                    copy_segments_far(layer)
                act.sem_inc(s_mark, 1)

            with act.Fori(0, L - 1) as layer:
                copy_segments(layer)
                act.wait_ge(s_sum, layer + 1)
                normed(layer * 2 + 1, ACT.Copy)
                act.wait_ge(s_var, layer + 2)
                nc.scalar.activation(bn_d[:], bn_m[:, 1:2], ACT.Sqrt, bias=eps[0:D, :]).then_inc(s_std, 1)
                act.wait_ge(s_bn, layer + 1)
                normed(layer * 2 + 2, bias=bn_b[:], scale=bn_a[:])
            copy_segments(L - 1)
            act.wait_ge(s_bn, L)
            normed(2 * L - 1)

        @block.tensor
        def _(pe):
            for _ in range(PICKED):
                pe.sem_inc(s_pick, 1)
            for _ in range(CREDIT):
                pe.sem_inc(s_root, 1)
                pe.sem_inc(s_seg, 1)
            pe.wait_ge(s_ident, 1)
            with pe.Fori(0, CHUNKS // SLOTS) as cb:
                for u in range(SLOTS):
                    pe.wait_ge(s_stage, cb * SLOTS + (u + 1))
                    if u >= TURNS:
                        pe.wait_ge(s_first, cb * SLOTS + (u - TURNS + 1))
                    for m in range(SUB):
                        last = nc.tensor.transpose(p_r[u % TURNS][:, m, :], stage[u][:, m, :],
                                                   ident[0:NODE_P, 0:NODE_P])
                    last.then_inc(s_chT, 1)
            pe.wait_ge(s_keyf, 1)
            flat = key_f.rearrange("p g j -> p (g j)")
            for c in range(PICKED):
                if c >= 2:
                    pe.wait_ge(s_key16, c - 1)
                nc.tensor.transpose(bank[c % 2][0:G, 0:P], flat[:, c * G:(c + 1) * G], ident[:]).then_inc(s_keyT, 1)
            pe.wait_ge(s_key16, PICKED)
            pe.wait_ge(s_base, 1)
            nc.tensor.transpose(bank[0][0:G, 0:P], low_p[:], ident[:]).then_inc(s_baseT, 1)
            pe.wait_ge(s_base, 2)
            nc.tensor.matmul(bank[1][:, 0:G], ones[0:G, :], low_d[:], start=True, stop=True).then_inc(s_baseT, 1)
            pe.wait_ge(s_base, 3)
            nc.tensor.transpose(bank[0][0:1, 0:P], far_p[:], ident[:]).then_inc(s_baseT, 1)
            pe.wait_ge(s_first, CHUNKS)

            def root_products(layer):
                pe.wait_ge(s_w, layer + 1)
                apart(pe)
                for c, u, n in node_chunks(pe, layer * 2 * CHUNKS):
                    pe.wait_ge(s_hT, n + 1)
                    pe.wait_ge(s_node, n + (CREDIT - 1))
                    apart(pe)
                    nc.tensor.matmul(p_r[u % TURNS], rw_now[:], hT[u][:], start=True, stop=True).then_inc(s_root, 1)

            root_products(0)

            def sum_tiles(products, onehots):
                for j in (*range(CUT - 1), *range(CUT, TILES), CUT - 1):
                    ends = dict(start=j == 0, stop=j == CUT - 1)
                    if j < CUT:
                        last = nc.tensor.matmul(p_parts, onehots[:, j, :],
                                                xparts[:, j, :, :].rearrange("p a b -> p (a b)"), **ends)
                    else:
                        nc.tensor.matmul(p_z, onehots[:, j, :].bitcast(F32), products[:, j, :], **ends)
                return last

            def sum_tiles_far(products, onehots):
                for j in range(TILES):
                    last = nc.tensor.matmul(p_z, onehots[:, j, :].bitcast(F32), products[:, j, :],
                                            start=j == 0, stop=j == TILES - 1)
                return last

            def transpose_sums():
                nc.tensor.transpose(p_zT, z[:, D:D + FD], ident[0:WIN, 0:WIN])
                return nc.tensor.transpose(p_zxT, z[:, 0:D], ident[0:WIN, 0:WIN])

            def messages():
                nc.tensor.matmul(p_agg, w_now[:], zT[:], start=True, stop=False)
                return nc.tensor.matmul(p_agg, eb_now[:], zxT[:], start=False, stop=True)

            def segment_sums_far(layer):
                with pe.Fori(0, G) as g:
                    pe.wait_ge(s_fprod, layer * G + g + 1)
                    apart(pe)
                    with pe.Fori(0, FAR) as w:
                        m = (layer * G + g) * FAR + w
                        pe.wait_ge(s_fhot, m + 1)
                        sum_tiles_far(xp[0], hot[0]).then_inc(s_fseg, 1)
                        pe.wait_ge(s_fz, m + 1)
                        transpose_sums().then_inc(s_fT, 1)
                        pe.wait_ge(s_fzT, m + 1)
                        messages().then_inc(s_fmm, 1)

            def pick(layer, b, u, t):
                k = layer * G + b * SLOTS + u
                if t % HALF == 0:
                    pe.wait_ge(s_low, k * 2 + (t // HALF + 1 + 2 * CREDIT))
                before = t - BANKS if t >= BANKS else max(range(t, PICKED, BANKS)) - PICKED
                pe.wait_ge(s_taken, k * PICKED + (before + 1 + PICKED))
                for f in range(FOLD):
                    for i in (1, 0):
                        last = nc.tensor.matmul(
                            p_sel[t % BANKS], low_hot[:, f, t, :],
                            nodes[i][:, f, :, :].rearrange("p f d -> p (f d)"),
                            start=(f, i) == (0, 1), stop=(f, i) == (FOLD - 1, 0))
                last.then_inc(s_pick, 1)

            def transposes_of(k):
                pe.wait_ge(s_z, k + 1)
                transpose_sums().then_inc(s_T, 1)

            def messages_of(k):
                pe.wait_ge(s_zT, k + 1)
                pe.wait_ge(s_add, k + CREDIT)
                messages().then_inc(s_mm, 1)

            def segment_sums(layer):
                pe.wait_ge(s_nodes, layer + 1)
                apart(pe)
                pe.wait_ge(s_node, (layer * 2 + 1) * CHUNKS + CREDIT)
                apart(pe)
                for t in range(PICKED):
                    pick(layer, 0, 0, t)
                for b, first, last in bodies(pe):
                    for u in range(SLOTS):
                        k = layer * G + b * SLOTS + u
                        for t in range(PICKED):
                            if not (last and u == SLOTS - 1):
                                pick(layer, b, u + 1, t)
                            if t == 3 and not (first and u == 0):
                                transposes_of(k - 1)
                            if t == 5 and not (first and u == 0):
                                messages_of(k - 1)
                        pe.wait_ge(s_hot, k + 1)
                        pe.wait_ge(s_xc, k + 1)
                        pe.wait_ge(s_prod, k + (1 + CREDIT))
                        pe.wait_ge(s_upper, k + 1)
                        pe.wait_ge(s_lower, k + 1)
                        sum_tiles(xp[u % PAIR], hot[u % PAIR]).then_inc(s_seg, 1)
                transposes_of(layer * G + (G - 1))
                messages_of(layer * G + (G - 1))
                far = farthest(pe)
                with pe.If(far > WIN - 1):
                    segment_sums_far(layer)
                pe.sem_inc(s_mark, 1)

            with pe.Fori(0, L - 1) as layer:
                segment_sums(layer)
                for c, u, n in node_chunks(pe, (layer * 2 + 1) * CHUNKS):
                    pe.wait_ge(s_hT, n + 1)
                    pe.wait_ge(s_node, n + (CREDIT - 1))
                    apart(pe)
                    for m in range(SUB):
                        last = nc.tensor.transpose(p_t[u % TURNS][:, m, :], hT[u][:, m, :], ident[0:D, 0:D])
                    last.then_inc(s_root, 1)
                pe.wait_ge(s_diag, layer + 1)
                apart(pe)
                nc.tensor.matmul(p_norm, ones[0:D, 0:NODE_P], bn_diag[:], start=True, stop=True).then_inc(s_norm, 1)
                root_products(layer + 1)
            segment_sums(L - 1)
            for c, u, n in node_chunks(pe, (2 * L - 1) * CHUNKS):
                pe.wait_ge(s_hT, n + 1)
                pe.wait_ge(s_node, n + (CREDIT - 1))
                apart(pe)
                for m in range(SUB):
                    last = nc.tensor.matmul(p_t[u % TURNS][:, m, :], hT[u][:, m, :], pw[:], start=True, stop=True)
                last.then_inc(s_root, 1)


def kernel(**inputs):
    import numpy as _np
    import concourse.bacc as _bacc
    from concourse import mybir as _mybir
    from concourse.bass_utils import run_bass_kernel_spmd as _run

    w = {k.removeprefix("L0_gnn_"): _np.asarray(v) for k, v in inputs.items()}
    laid = {
        "x": w["x"], "src": w["src"], "dst": w["dst"], "edge_attr": w["edge_attr_8"],
        "edge_w": w["edge_w"], "edge_b": w["edge_b"], "root_w": w["root_w"],
        "root_b": w["root_b"].T, "gamma": w["bn_gamma"].T, "beta": w["bn_beta"].T,
        "pred_w": w["pred_w"], "pred_b": w["pred_b"],
    }
    nc = _bacc.Bacc("TRN2", target_bir_lowering=False, num_devices=1)
    arrays, args = {}, []
    for name, a in laid.items():
        a = _np.ascontiguousarray(a)
        arrays[f"in_{name}"] = a
        args.append(nc.dram_tensor(f"in_{name}", a.shape, _mybir.dt.from_np(a.dtype), kind="ExternalInput").ap())
    o = nc.dram_tensor("out_x", w["x"].shape, _mybir.dt.float32, kind="ExternalOutput").ap()
    gnn_kernel(nc, *args, o)
    r = _run(nc, [arrays], core_ids=[0])
    return r.results[0]["out_x"]
```
